# Optimizing a Trainium2 kernel written in Bass

```python
import numpy as np
import jax
import jax.numpy as jnp

def _softmax(x, axis=-1):
    return jax.nn.softmax(x, axis=axis)

def _gelu(x):
    return jax.nn.gelu(x, approximate=True)

def _silu(x):
    return jax.nn.silu(x)

def _sigmoid(x):
    return jax.nn.sigmoid(x)

def _layernorm(x, axis=-1, eps=1e-05):
    m = jnp.mean(x, axis=axis, keepdims=True)
    v = jnp.var(x, axis=axis, keepdims=True)
    return (x - m) / jnp.sqrt(v + eps)

def _scatter_add(tgt, idx, src, axis=0):
    return tgt.at[idx].add(src)

def _segment_sum(src, seg, n):
    return jax.ops.segment_sum(src, seg, n)
kernel_name = 'mk_gnn_ffn_d1_gnn_r32_57d9bd'

def setup_inputs(seed: int=0):
    np.random.seed(seed)
    _w = jnp.asarray

    def _rec_inputs():
        import jax
        import jax.numpy as jnp
        _gk = jax.random.key(seed)
        x = -8.776e-05 + 1 * jax.random.normal(jax.random.fold_in(_gk, 1), (3125, 256), jnp.float32)
        _s = jax.random.randint(jax.random.fold_in(_gk, 2), (25000,), 0, 3125, jnp.int32)
        _d = jax.random.randint(jax.random.fold_in(_gk, 3), (25000,), 0, 3125, jnp.int32)
        _loop = jnp.arange(3125, dtype=jnp.int32)
        src = jnp.concatenate([_s, _d, _loop])
        dst = jnp.concatenate([_d, _s, _loop])
        _o = jnp.argsort(dst, stable=True)
        src = src[_o]
        dst = dst[_o]
        edge_type_16 = jax.random.randint(jax.random.fold_in(_gk, 12), (53125,), 0, 16, jnp.int32)
        edge_weight1 = jax.random.uniform(jax.random.fold_in(_gk, 13), (53125, 1), jnp.float32, 0.0, 0.999998)
        return (x, src, dst, edge_type_16, edge_weight1)
    x, src, dst, edge_type_16, edge_weight1 = _rec_inputs()

    def _L0_gnn_setup():
        import jax, jax.numpy as jnp
        import numpy as np
        N_NODES = 625
        N_EDGES = 10000
        NUM_RELS = 16
        IN_FEAT = 256
        OUT_FEAT = 256
        key = jax.random.key(seed)
        k_h, k_w, k_n, k_s, k_d, k_r = jax.random.split(key, 6)
        h = jax.random.normal(k_h, (N_NODES, IN_FEAT), dtype=jnp.float32)
        weight = jax.random.normal(k_w, (NUM_RELS, IN_FEAT, OUT_FEAT), dtype=jnp.float32)
        norm = jax.random.uniform(k_n, (N_EDGES, 1), dtype=jnp.float32)
        src = jax.random.randint(k_s, (N_EDGES,), 0, N_NODES, dtype=jnp.int32)
        dst = jax.random.randint(k_d, (N_EDGES,), 0, N_NODES, dtype=jnp.int32)
        rel_type = jax.random.randint(k_r, (N_EDGES,), 0, NUM_RELS, dtype=jnp.int32)
        return {'h': h, 'weight': weight, 'norm': norm, 'src': src, 'dst': dst, 'rel_type': rel_type}
    _L0_gnn_all = _L0_gnn_setup()
    _L0_gnn_in = {k: v for k, v in _L0_gnn_all.items() if k in ('weight',)}
    del _L0_gnn_all

    def _L0_ffn_setup():
        import math
        import jax, jax.numpy as jnp
        import numpy as np
        CAPACITY_FACTOR = 1.25
        TOP_K = 2
        LN_EPS = 1e-05

        def _layer_norm(x, gamma, beta):
            mu = jnp.mean(x, axis=-1, keepdims=True)
            var = jnp.var(x, axis=-1, keepdims=True)
            return (x - mu) * jax.lax.rsqrt(var + LN_EPS) * gamma + beta
        key = jax.random.key(seed)
        ks = jax.random.split(key, 4)
        B, S, D, F, E = (8, 128, 256, 512, 8)
        x = jax.random.normal(ks[0], (B, S, D), dtype=jnp.float32)
        Wr = jax.random.normal(ks[1], (D, E), dtype=jnp.float32) / np.sqrt(D)
        br = jnp.zeros((E,), jnp.float32)
        W1 = jax.random.normal(ks[2], (E, D, F), dtype=jnp.float32) / np.sqrt(D)
        b1 = jnp.zeros((E, F), jnp.float32)
        W2 = jax.random.normal(ks[3], (E, F, D), dtype=jnp.float32) / np.sqrt(F)
        b2 = jnp.zeros((E, D), jnp.float32)
        gamma = jnp.ones((D,), jnp.float32)
        beta = jnp.zeros((D,), jnp.float32)
        return {'x': x, 'Wr': Wr, 'br': br, 'W1': W1, 'b1': b1, 'W2': W2, 'b2': b2, 'gamma': gamma, 'beta': beta}
    _L0_ffn_all = _L0_ffn_setup()
    _L0_ffn_in = {k: v for k, v in _L0_ffn_all.items() if k in ('Wr', 'br', 'W1', 'b1', 'W2', 'b2', 'gamma', 'beta')}
    del _L0_ffn_all
    return {'x': x, 'src': src, 'dst': dst, 'edge_type_16': edge_type_16, 'edge_weight1': edge_weight1, 'L0_gnn_weight': _L0_gnn_in['weight'], 'L0_ffn_Wr': _L0_ffn_in['Wr'], 'L0_ffn_br': _L0_ffn_in['br'], 'L0_ffn_W1': _L0_ffn_in['W1'], 'L0_ffn_b1': _L0_ffn_in['b1'], 'L0_ffn_W2': _L0_ffn_in['W2'], 'L0_ffn_b2': _L0_ffn_in['b2'], 'L0_ffn_gamma': _L0_ffn_in['gamma'], 'L0_ffn_beta': _L0_ffn_in['beta']}

def reference(x, src, dst, edge_type_16, edge_weight1, L0_gnn_weight, L0_ffn_Wr, L0_ffn_br, L0_ffn_W1, L0_ffn_b1, L0_ffn_W2, L0_ffn_b2, L0_ffn_gamma, L0_ffn_beta):
    import jax
    import jax.numpy as jnp

    def _L0_gnn_ref(h, weight, norm, src, dst, rel_type):
        import jax, jax.numpy as jnp
        import numpy as np
        N_NODES = 625
        N_EDGES = 10000
        NUM_RELS = 16
        IN_FEAT = 256
        OUT_FEAT = 256
        transformed = jnp.einsum('ni,rio->rno', h, weight)
        msg = transformed[rel_type, src] * norm
        out = jax.ops.segment_sum(msg, dst, num_segments=h.shape[0])
        return out

    def _L0_ffn_ref(x, Wr, br, W1, b1, W2, b2, gamma, beta):
        import math
        import jax, jax.numpy as jnp
        import numpy as np
        CAPACITY_FACTOR = 1.25
        TOP_K = 2
        LN_EPS = 1e-05

        def _layer_norm(x, gamma, beta):
            mu = jnp.mean(x, axis=-1, keepdims=True)
            var = jnp.var(x, axis=-1, keepdims=True)
            return (x - mu) * jax.lax.rsqrt(var + LN_EPS) * gamma + beta
        B, S, D = x.shape
        E = Wr.shape[1]
        N = B * S
        K = TOP_K
        logits = jnp.mean(x, axis=1) @ Wr + br
        routing_weights = jax.nn.softmax(logits, axis=-1)
        capacity = float(math.ceil(N * CAPACITY_FACTOR / E))
        expected_loads = routing_weights.sum(axis=0) * (N / B)
        scale = jnp.where(expected_loads > capacity, capacity / expected_loads, 1.0)
        routing_weights = jax.nn.softmax(routing_weights * scale, axis=-1)
        rw_tok = jnp.broadcast_to(routing_weights[:, None, :], (B, S, E)).reshape(N, E)
        top_w, top_i = jax.lax.top_k(rw_tok, K)
        top_w = jax.nn.softmax(top_w, axis=-1)
        xf = x.reshape(N, D)
        h = jax.nn.gelu(jnp.einsum('nd,edf->enf', xf, W1) + b1[:, None, :], approximate=False)
        y = jnp.einsum('enf,efd->end', h, W2) + b2[:, None, :]
        w_dense = jnp.zeros((N, E), x.dtype).at[jnp.arange(N)[:, None], top_i].add(top_w)
        out = jnp.einsum('ne,end->nd', w_dense, y).reshape(B, S, D)
        out = _layer_norm(out + x, gamma, beta)
        return out
    x = x + _L0_gnn_ref(_layernorm(x, axis=-1), L0_gnn_weight, edge_weight1, src, dst, edge_type_16)
    x = x + _L0_ffn_ref(_layernorm(x, axis=-1)[None], L0_ffn_Wr, L0_ffn_br, L0_ffn_W1, L0_ffn_b1, L0_ffn_W2, L0_ffn_b2, L0_ffn_gamma, L0_ffn_beta)[0]
    return x

_drawn_inputs = setup_inputs


def setup_inputs(seed=0):
    import zlib

    import numpy as np

    out = dict(_drawn_inputs(seed))
    spreads = {'L0_ffn_br': (0.0, 0.713),
     'L0_ffn_b1': (0.0, 2.0),
     'L0_ffn_b2': (0.0, 2.0),
     'L0_ffn_gamma': (1.0, 0.6),
     'L0_ffn_beta': (0.0, 2.0)}
    factors = {'L0_ffn_Wr': 8.0, 'L0_ffn_W1': 5.682, 'L0_ffn_W2': 5.175}
    for name, (base, spread) in spreads.items():
        noise = np.random.default_rng([zlib.crc32(name.encode()), seed]).standard_normal(out[name].shape)
        drawn = base * np.exp(spread * noise) if base else spread * noise
        out[name] = jnp.asarray(drawn.astype(out[name].dtype))
    for name, factor in factors.items():
        out[name] = (out[name] * factor).astype(out[name].dtype)
    return out
```

```python
import numpy as np
import concourse.bass as bass
from concourse import mybir
from contextlib import ExitStack

F32 = mybir.dt.float32
F32R = mybir.dt.float32r
I32 = mybir.dt.int32
U32 = mybir.dt.uint32
ALU = mybir.AluOpType
ACT = mybir.ActivationFunctionType
AX = mybir.AxisListType

P = 128
N_NODES, D = 3125, 256
N_RELS = 16
N_EDGES = 53125
N_EXPERTS, D_FF, TOP_K = 8, 512, 2
LN_EPS = 1e-5
CAPACITY = float(-(-N_NODES * 5 // (4 * N_EXPERTS)))

KH = D // P
NT = -(-N_NODES // P)
LAST = N_NODES - (NT - 1) * P
TROW = N_RELS * D
NCG = TROW // 512

CHUNK = 512
NCH = -(-N_EDGES // CHUNK)
CT = CHUNK // P
TAIL = N_EDGES - (NCH - 1) * CHUNK
SLOTS = 4
WIN = 64
NO_NODE = 1 << 20
FBW = 400
NFB = -(-NT * P // FBW)

TG = 2 * P
NG = -(-NT * P // TG)
NF = D_FF // P
NQ = TOP_K * NF
NU = NQ // 2
ACOLS = NG * TG
LG = 5
NLG = NT // LG
assert NT % 2 == 1 and NT == NLG * LG and NCH % SLOTS == 0 and NG == 13


def gnn_ffn(nc, x_in, src_in, dst_in, rel_in, norm_in, w_in, wr_in, br_in, w1_in, b1_in, w2_in, b2_in,
            gamma_in, beta_in, out):
    table = nc.dram_tensor("table", [NT * P * N_RELS, D], F32, kind="Internal").ap()
    table_tiles = table.rearrange("(t p r) d -> t p (r d)", p=P, r=N_RELS)

    ctx = ExitStack()
    with ctx:
        base = [16512]

        def region(nbytes):
            at = base[0]
            base[0] = at + -(-nbytes // 32) * 32
            assert base[0] <= nc.sbuf_usable_end, base[0]
            return at

        def at(name, shape, dtype, offset):
            return nc.alloc_sbuf_tensor_at(name, shape, dtype, offset=offset)

        def sb(name, shape, dtype=F32):
            return at(name, shape, dtype, region(4 * int(np.prod(shape[1:]))))

        def sem(name):
            return ctx.enter_context(nc.semaphore(name))

        x = sb("x", [P, NT, D])
        acc = sb("acc", [P, KH, ACOLS])
        ident = sb("ident", [P, P])
        minus_half = sb("minus_half", [P, LG])
        eps = sb("eps", [P, LG])
        gamma = sb("gamma", [P, D])
        beta = sb("beta", [P, D])
        wr = sb("wr", [P, KH, N_EXPERTS])
        b1t = sb("b1t", [P, N_EXPERTS * NF])
        b1s = sb("b1s", [P, NQ])
        stat = sb("stat", [P, LG, 6])
        mv1 = sb("mv1", [P, 2, 2])
        var_eps = sb("var_eps", [P, LG])
        rstd1 = sb("rstd1", [P, NT])
        mv2 = sb("mv2", [P, NT, 2])
        rstd2 = sb("rstd2", [P, NT])
        mv2_now = sb("mv2_now", [P, LG, 2])
        mv3 = sb("mv3", [P, 2, 2, 2])
        rstd3 = sb("rstd3", [P, 2 * NG])
        iota_i = sb("iota_i", [P, WIN], I32)
        iota = sb("iota", [P, WIN])
        idx_col = sb("idx_col", [P, NCH, CT], I32)
        norm_col = sb("norm_col", [P, NCH, CT])
        idx_now = sb("idx_now", [P, SLOTS, CT], I32)
        w0_row = sb("w0_row", [1, NCH + 1], I32)
        xn = sb("xn", [P, D])
        ht_hi = sb("ht_hi", [P, 2, D], F32R)
        ht_lo = sb("ht_lo", [P, 2, D], F32R)
        acc_stage = sb("acc_stage", [P, 3, D])
        xs_hi = sb("xs_hi", [P, 2, KH, TG], F32R)
        xs_lo = sb("xs_lo", [P, 2, KH, TG], F32R)
        g = sb("g", [P, 2, 2, TG])

        r_big = region(65536)
        w_hi = at("w_hi", [P, NCG, KH, 512], F32R, r_big)
        w_lo = at("w_lo", [P, NCG, KH, 512], F32R, r_big + 32768)
        w1_hi = at("w1_hi", [P, TOP_K, KH, D_FF], F32R, r_big)
        w1_lo = at("w1_lo", [P, TOP_K, KH, D_FF], F32R, r_big + 8192)
        w2_hi = at("w2_hi", [P, NQ, D], F32R, r_big + 16384)
        w2_lo = at("w2_lo", [P, NQ, D], F32R, r_big + 24576)
        g_hi = at("g_hi", [P, 2, NQ, TG], F32R, r_big + 32768)
        g_lo = at("g_lo", [P, 2, NQ, TG], F32R, r_big + 49152)
        xn_group = at("xn_group", [P, LG, D], F32, r_big)
        r_cols = region(4096)
        rel_pos = at("rel_pos", [P, NCH, CT], F32, r_cols)
        dst_col = at("dst_col", [P, NCH, CT], F32, r_cols + 1664)
        z = at("z", [P, 2, 2, D], F32, r_cols)
        r_sel = region(4096)
        sel = at("sel", [P, SLOTS, CT, WIN], F32, r_sel)
        o = at("o", [P, 2, 2, D], F32, r_sel)
        r_stage = region(32768)
        w_raw = at("w_raw", [P, NCG, KH, 512], F32, r_stage)
        t_stage = at("t_stage", [P, 2, TROW], F32, r_stage)
        xl = at("xl", [P, 2 * NG, D], F32, r_stage)
        fb_iota = at("fb_iota", [P, NFB, FBW], F32, r_stage + 1600)
        fb_sel = at("fb_sel", [P, CT, FBW], F32, r_stage + 1600 + 12800)
        fb_norm = at("fb_norm", [P, NCH, CT], F32, r_stage + 1600 + 12800 + 6400)
        r_gather = region(16384)
        gath = at("gath", [P, SLOTS, CT, D], F32, r_gather)
        src_rows = at("src_rows", [NCH, CHUNK], I32, r_gather)
        rel_rows = at("rel_rows", [NCH, CHUNK], I32, r_gather + 2048)
        dst_rows = at("dst_rows", [NCH, CHUNK], I32, r_gather + 4096)
        norm_rows = at("norm_rows", [NCH, CHUNK], F32, r_gather + 6144)
        srcf_rows = at("srcf_rows", [NCH, CHUNK], F32, r_gather + 8192)
        idxf_rows = at("idxf_rows", [NCH, CHUNK], F32, r_gather + 10240)
        dstf_rows = at("dstf_rows", [NCH, CHUNK], F32, r_gather + 12288)
        relf_rows = at("relf_rows", [NCH, CHUNK], F32, r_gather + 14336)
        w1_raw = at("w1_raw", [P, TOP_K, KH, D_FF], F32, r_gather)
        w2_raw = at("w2_raw", [P, NQ, D], F32, r_gather + 8192)
        b1_rows = sb("b1_rows", [N_EXPERTS * NF, P])
        w0_rows = sb("w0_rows", [NCH, 2])
        ones = sb("ones", [P, P])
        mean_sum = sb("mean_sum", [P, KH, NT])
        mean = sb("mean", [P, KH])
        rt = sb("rt", [1, 16, N_EXPERTS])
        top_i = sb("top_i", [1, 8], U32)
        b2_pair = sb("b2_pair", [1, TOP_K, D])
        w_rows = sb("w_rows", [1, TOP_K, P])
        w_cols = sb("w_cols", [P, TOP_K])
        b2c = sb("b2c", [P, D])
        br = sb("br", [1, N_EXPERTS])

        pos_rows = at("pos_rows", [NCH, CHUNK], F32, r_gather + 2048)
        miss_rows = at("miss_rows", [NCH, CHUNK], F32, r_gather)

        RING = [0, 1, 0, 1, 2]
        bank = [ctx.enter_context(nc.psum_tensor(f"bank{i}", [P, 512], F32)) for i in range(8)]

        ACC_BANKS, XL_BANKS = [bank[0], bank[1], bank[5]], [bank[2], bank[3], bank[6]]

        x0_in, x_in_sem, edges_in, consts_in = sem("x0_in"), sem("x_in"), sem("edges_in"), sem("consts_in")
        bc_in = sem("bc_in")
        w_in_sem = [sem(f"w_in{c}") for c in range(NCG)]
        x_zeroed, rows_filled, ident_ready = sem("x_zeroed"), sem("rows_filled"), sem("ident_ready")
        pool_step = sem("pool_step")
        consts_ready = sem("consts_ready")
        whi_ready, wlo_even, wlo_odd = sem("whi_ready"), sem("wlo_even"), sem("wlo_odd")
        stat_ready, mv_ready, rstd_ready, xn_ready = sem("stat_ready"), sem("mv_ready"), sem("rstd_ready"), sem("xn_ready")
        tp_ready, hthi_ready, htlo_ready = sem("tp_ready"), sem("hthi_ready"), sem("htlo_ready")
        mm_done, even_out, odd_out = sem("mm_done"), sem("even_out"), sem("odd_out")
        t_written = [sem("t_written0"), sem("t_written1")]
        edge_math, dve_meta, meta_tp, meta_copied = sem("edge_math"), sem("dve_meta"), sem("meta_tp"), sem("meta_copied")
        idx_copied, acc_zeroed = sem("idx_copied"), sem("acc_zeroed")
        idx_now_ready = sem("idx_now_ready")
        gathered = [sem(f"gathered{k}") for k in range(SLOTS)]
        sel_ready, chunk_summed, acc_added = sem("sel_ready"), sem("chunk_summed"), sem("acc_added")
        fb_step, fb_sel_ready, fb_summed, fb_added, fb_gathered = (
            sem("fb_step"), sem("fb_sel_ready"), sem("fb_summed"), sem("fb_added"), sem("fb_gathered"))
        acc_final = sem("acc_final")
        staged, acc_tp, x1_ready = sem("staged"), sem("acc_tp"), sem("x1_ready")
        stat2_ready, mv2_ready, rstd2_ready = sem("stat2_ready"), sem("mv2_ready"), sem("rstd2_ready")
        xng_ready, xl_tp, xlt_ready, xl_ready = sem("xng_ready"), sem("xl_tp"), sem("xlt_ready"), sem("xl_ready")
        mean_ready, logits_ready, route, exp_done = sem("mean_ready"), sem("logits_ready"), sem("route"), sem("exp_done")
        idx_ready = sem("idx_ready")
        w1_got = [sem(f"w1_got{e}") for e in range(TOP_K)]
        w2_got = [sem(f"w2_got{e}") for e in range(TOP_K)]
        b2_got = sem("b2_got")
        wts_ready, wcol_ps, wcol_ready, b2_ps, b2_ready = (
            sem("wts_ready"), sem("wcol_ps"), sem("wcol_ready"), sem("b2_ps"), sem("b2_ready"))
        b1_tp, b1t_ready, b1s_ready = sem("b1_tp"), sem("b1t_ready"), sem("b1s_ready")
        w1hi_ready, w1lo_ready, w2s_ready, w2hi_ready, w2lo_ready = (
            sem("w1hi_ready"), sem("w1lo_ready"), sem("w2s_ready"), sem("w2hi_ready"), sem("w2lo_ready"))
        xshi_ready, xslo_ready = sem("xshi_ready"), sem("xslo_ready")
        ffn1_done, gelu_done, ghi_ready, glo_ready = sem("ffn1_done"), sem("gelu_done"), sem("ghi_ready"), sem("glo_ready")
        ffn2_done, xlb_ready, z_ready, stat3_ready, mv3_ready = (
            sem("ffn2_done"), sem("xlb_ready"), sem("z_ready"), sem("stat3_ready"), sem("mv3_ready"))
        rstd3_ready, zn_ready, o_ready = sem("rstd3_ready"), sem("zn_ready"), sem("o_ready")
        fin_step = sem("fin_step")
        out_written = [sem("out_written0"), sem("out_written1")]

        block = ctx.enter_context(nc.Block())

        def nop_waits(engine):
            engine.nop(nofuse=True)

        def flat(a):
            return a.rearrange("(c e) -> c e", e=CHUNK)

        @block.sync
        def _(sp):
            sp.dma_start(x[:, 0, :], x_in[0:P, :]).then_inc(x0_in, 16)
            for c in range(NCG):
                for kh in range(KH):
                    sp.dma_start(w_raw[:, c, kh, :].rearrange("p (r o) -> p r o", r=2),
                                 w_in[2 * c:2 * c + 2, kh * P:(kh + 1) * P, :].rearrange("r p o -> p r o")
                                 ).then_inc(w_in_sem[c], 16)
            sp.dma_start(x[:, 1:NT - 1, :],
                         x_in[P:(NT - 1) * P, :].rearrange("(t p) d -> p t d", p=P)).then_inc(x_in_sem, 16)
            sp.wait_ge(x_zeroed, 1)
            full = LAST // 16 * 16
            sp.dma_start(x[0:full, NT - 1, :], x_in[(NT - 1) * P:(NT - 1) * P + full, :]).then_inc(x_in_sem, 16)
            sp.dma_start(x[full:LAST, NT - 1, :], x_in[(NT - 1) * P + full:N_NODES, :]).then_inc(x_in_sem, 16)
            def store_table(t, b):
                sp.wait_ge(even_out, NCG // 2 * (t + 1) + 2)
                sp.wait_ge(odd_out, NCG // 2 * (t + 1) + 2)
                sp.dma_start(table_tiles[t], t_stage[:, b, :]).then_inc(t_written[b], 16)

            with sp.Fori(0, NT // 2) as i:
                for b in range(2):
                    store_table(2 * i + b, b)
            store_table(NT - 1, 0)

            sp.wait_ge(idx_ready, 1)
            for k in range(TOP_K):
                e = sp.value_load(top_i[0:1, k:k + 1], min_val=0, max_val=N_EXPERTS - 1)
                sp.dma_start(w1_raw[:, k, :, :], w1_in.rearrange("e (h p) f -> e p h f", p=P)[e]
                             ).then_inc(w1_got[k], 16)
                sp.dma_start(w2_raw[:, k * NF:(k + 1) * NF, :], w2_in.rearrange("e (j p) d -> e p j d", p=P)[e]
                             ).then_inc(w2_got[k], 16)
                sp.dma_start(b2_pair[0:1, k, :], b2_in[bass.ds(e, 1), :]).then_inc(b2_got, 16)

            def store_out(gi, b, full_group):
                sp.wait_ge(o_ready, gi + 1)
                if full_group:
                    sp.dma_start(out[bass.ds(gi * TG, TG), :].rearrange("(s p) d -> p s d", p=P),
                                 o[:, b, :, :]).then_inc(out_written[b], 16)
                else:
                    sp.dma_start(out[gi * TG:gi * TG + full, :], o[0:full, b, 0, :]).then_inc(out_written[b], 16)
                    sp.dma_start(out[gi * TG + full:N_NODES, :], o[full:LAST, b, 0, :]).then_inc(out_written[b], 16)

            with sp.Fori(0, NG // 2) as i:
                for b in range(2):
                    store_out(2 * i + b, b, True)
            store_out(NG - 1, 0, False)
            sp.wait_ge(out_written[0], 16 * (NG // 2) + 32)
            sp.wait_ge(out_written[1], 16 * (NG // 2))

        @block.gpsimd
        def _(pool):
            steps = [0]

            def after(ins):
                steps[0] += 1
                ins.then_inc(pool_step, 1)
                pool.wait_ge(pool_step, steps[0])

            nc.gpsimd.memset(x[:, NT - 1, :], 0.0).then_inc(x_zeroed, 1)
            pool.wait_ge(x_zeroed, 1)
            lo = NCH // 32 * 32
            nc.gpsimd.memset(src_rows[lo:NCH, :], 0).then_inc(rows_filled, 1)
            nc.gpsimd.memset(rel_rows[lo:NCH, :], 0).then_inc(rows_filled, 1)
            nc.gpsimd.memset(norm_rows[lo:NCH, :], 0.0).then_inc(rows_filled, 1)
            nc.gpsimd.memset(dst_rows[lo:NCH, :], NO_NODE).then_inc(rows_filled, 1)
            pool.wait_ge(rows_filled, 4)
            after(nc.gpsimd.memset(ident[:], 0.0))
            nc.gpsimd.affine_select(out=ident[:], in_=ident[:], compare_op=ALU.not_equal, fill=1.0, base=0,
                                    pattern=[[-1, P]], channel_multiplier=1).then_inc(ident_ready, 1)
            after(nc.gpsimd.memset(minus_half[:], -0.5))
            after(nc.gpsimd.memset(eps[:], LN_EPS))

            def rstd_pool(var, out_ap, n, half, ready, step_at):
                nc.gpsimd.tensor_tensor(var_eps[:, 0:n], var, eps[:, 0:n], ALU.add).then_inc(pool_step, 1)
                pool.wait_ge(pool_step, step_at)
                nc.gpsimd.tensor_tensor(out_ap, var_eps[:, 0:n], half, ALU.pow).then_inc(ready, 1)

            pool.wait_ge(mv_ready, 1)
            steps[0] += 1
            rstd_pool(mv1[:, 0, 1:2], rstd1[:, 0:1], 1, minus_half[:, 0:1], rstd_ready, steps[0])
            for c in range(1, NCG, 2):
                pool.wait_ge(w_in_sem[c], 16 * KH)
                pool.wait_ge(whi_ready, c + 1)
                nc.gpsimd.tensor_tensor(w_lo[:, c, :, :], w_raw[:, c, :, :], w_hi[:, c, :, :].bitcast(F32),
                                        ALU.subtract).then_inc(wlo_odd, 1)
            pool.wait_ge(mv_ready, 2)
            pool.wait_ge(rstd_ready, 1)
            steps[0] += 1
            rstd_pool(mv1[:, 1, 1:2], rstd1[:, 1:2], 1, minus_half[:, 0:1], rstd_ready, steps[0])
            nc.gpsimd.memset(ones[:], 1.0)
            nc.gpsimd.iota(iota_i[:], [[1, WIN]], base=0, channel_multiplier=0).then_inc(consts_ready, 1)
            pool.wait_ge(consts_ready, 1)
            nc.gpsimd.tensor_copy(iota[:], iota_i[:]).then_inc(consts_ready, 1)
            base_steps = steps[0]

            def rstd_tile(t, b):
                pool.wait_ge(mv_ready, t + 1)
                pool.wait_ge(rstd_ready, t)
                rstd_pool(mv1[:, b, 1:2], rstd1[:, bass.ds(t, 1)], 1, minus_half[:, 0:1], rstd_ready,
                          t + (base_steps - 1))

            with pool.Fori(0, (NT - 3) // 2) as i:
                rstd_tile(2 * i + 2, 0)
                rstd_tile(2 * i + 3, 1)
            rstd_tile(NT - 1, 0)
            steps[0] = base_steps + (NT - 2)
            nc.gpsimd.memset(acc[:], 0.0).then_inc(acc_zeroed, 1)
            pool.wait_ge(edges_in, 4 * 3 * 16)
            nc.gpsimd.tensor_copy(srcf_rows[:], src_rows[:])
            nc.gpsimd.tensor_copy(relf_rows[:], rel_rows[:])
            after(nc.gpsimd.tensor_copy(dstf_rows[:], dst_rows[:]))
            after(nc.gpsimd.tensor_scalar(idxf_rows[:], srcf_rows[:], float(N_RELS), 0.0, ALU.mult, ALU.add))
            nc.gpsimd.tensor_tensor(idxf_rows[:], idxf_rows[:], relf_rows[:], ALU.add).then_inc(edge_math, 1)

            pool.wait_ge(t_written[0], 16 * (NT // 2 + 1))
            pool.wait_ge(t_written[1], 16 * (NT // 2))
            pool.wait_ge(meta_tp, 4)

            def gather(slot, signal):
                nop_waits(pool)
                for j in range(CT):
                    nc.gpsimd.indirect_dma_start(
                        out=gath[:, slot, j, :], out_offset=None, in_=table,
                        in_offset=bass.IndirectOffsetOnAxis(ap=idx_now[:, slot, j:j + 1], axis=0)
                    ).then_inc(signal, 16)

            with pool.Fori(0, NCH // SLOTS) as i:
                for k in range(SLOTS):
                    pool.wait_ge(idx_now_ready, i * SLOTS + k + 1)
                    pool.wait_ge(chunk_summed, i * SLOTS + k + 1)
                    gather(k, gathered[k])

            pool.wait_ge(meta_copied, 5)
            for k in range(SLOTS):
                pool.wait_ge(gathered[k], 64 * (NCH // SLOTS))
            pool.wait_ge(chunk_summed, NCH + SLOTS)
            missed = pool.value_load(w0_row[0:1, NCH:NCH + 1], min_val=0, max_val=1)
            with pool.If(missed):
                with pool.Fori(0, NCH) as c:
                    pool.wait_ge(fb_summed, c * NFB)
                    nc.gpsimd.tensor_copy(idx_now[:, 0, :], idx_col[:, bass.ds(c, 1), :].rearrange("p a b -> p (a b)")
                                          ).then_inc(fb_step, 1)
                    pool.wait_ge(fb_step, c + 1)
                    gather(0, fb_gathered)
                    pool.wait_ge(fb_gathered, c * 64 + 64)

            base_steps = steps[0]

            def rstd_group(gi):
                pool.wait_ge(mv2_ready, gi + 1)
                pool.wait_ge(rstd2_ready, gi)
                rstd_pool(mv2[:, bass.ds(gi * LG, LG), 1], rstd2[:, bass.ds(gi * LG, LG)], LG, minus_half[:],
                          rstd2_ready, gi + (base_steps + 1))

            def keep_xl(gi):
                for j in range(LG):
                    pool.wait_ge(xng_ready, gi * LG + j + 1)
                    last = nc.gpsimd.tensor_copy(xl[:, bass.ds(gi * LG + j, 1), :].rearrange("p a b -> p (a b)"),
                                                 xn_group[:, j, :])
                    last.then_inc(xl_ready, 1)

            pool.wait_ge(acc_final, 1)
            rstd_group(0)
            with pool.Fori(0, NLG - 1) as gi:
                rstd_group(gi + 1)
                keep_xl(gi)
            keep_xl(NLG - 1)
            steps[0] = base_steps + NLG

            def add_b2(gi, n):
                cols = xl[:, bass.ds(gi * 2, n), :]
                nc.gpsimd.tensor_tensor(cols, cols, b2c[:].unsqueeze(1).to_broadcast([P, n, D]), ALU.add
                                        ).then_inc(xlb_ready, 1)

            def rstd_out(gi, b, n, step_at):
                pool.wait_ge(mv3_ready, gi + 1)
                rstd_pool(mv3[:, b, 0:n, 1], rstd3[:, bass.ds(gi * 2, n)], n, minus_half[:, 0:n],
                          rstd3_ready, step_at)

            def finish(gi, b, n):
                pool.wait_ge(zn_ready, gi + 1)
                pool.wait_ge(out_written[b], gi * 8 - (8 * b))
                zb, ob = z[:, b, 0:n, :], o[:, b, 0:n, :]
                bc = lambda a: a[:].unsqueeze(1).to_broadcast([P, n, D])
                nc.gpsimd.tensor_tensor(ob, zb, bc(gamma), ALU.mult).then_inc(fin_step, 1)
                pool.wait_ge(fin_step, gi * 2 + 1)
                nc.gpsimd.tensor_tensor(ob, ob, bc(beta), ALU.add).then_inc(fin_step, 1)
                pool.wait_ge(fin_step, gi * 2 + 2)
                nc.gpsimd.tensor_tensor(ob, ob, x[:, bass.ds(gi * 2, n), :], ALU.add).then_inc(o_ready, 1)

            pool.wait_ge(xlt_ready, KH * (NT + 2))
            nc.gpsimd.tensor_copy(xs_hi[:, 0, :, :], acc[:, :, 0:TG]).then_inc(xshi_ready, 1)
            nc.gpsimd.tensor_copy(xs_hi[:, 1, :, :], acc[:, :, TG:2 * TG]).then_inc(xshi_ready, 1)
            for k in range(TOP_K):
                pool.wait_ge(w2hi_ready, k + 1)
                half = slice(k * NF, k * NF + NF)
                nc.gpsimd.tensor_tensor(w2_lo[:, half, :], w2_raw[:, half, :], w2_hi[:, half, :].bitcast(F32),
                                        ALU.subtract).then_inc(w2lo_ready, 1)
            pool.wait_ge(b2_ready, 1)
            pool.wait_ge(bc_in, 32)
            pool.wait_ge(xl_ready, NT)
            add_b2(0, 2)
            base_steps = steps[0]

            def step(gi, b, first=False):
                if not isinstance(gi, int) or gi + 2 < NG:
                    pool.wait_ge(ffn1_done, gi * NU + NU)
                    nc.gpsimd.tensor_copy(xs_hi[:, b, :, :], acc[:, :, bass.ds(gi * TG + 2 * TG, TG)]
                                          ).then_inc(xshi_ready, 1)
                if not isinstance(gi, int) or gi + 1 < NG:
                    add_b2(gi + 1, 1 if isinstance(gi, int) and gi + 1 == NG - 1 else 2)
                if not first:
                    finish(gi - 1, 1 - b, 2)
                rstd_out(gi, b, 1 if isinstance(gi, int) and gi == NG - 1 else 2, gi + (base_steps + 1))

            step(0, 0, first=True)
            with pool.Fori(0, 5) as i:
                step(2 * i + 1, 1)
                step(2 * i + 2, 0)
            step(11, 1)
            step(12, 0)
            finish(12, 0, 1)

        @block.scalar
        def _(act):
            act.sem_inc(even_out, 2)
            act.sem_inc(xlt_ready, 2 * KH)
            act.sem_inc(gelu_done, NU)
            act.wait_ge(rows_filled, 4)
            for rows, src in ((src_rows, src_in), (rel_rows, rel_in), (dst_rows, dst_in),
                              (norm_rows, norm_in.rearrange("e one -> (e one)"))):
                lo, full = NCH // 32 * 32, NCH - 1
                act.dma_start(rows[0:lo, :], flat(src[0:lo * CHUNK])).then_inc(edges_in, 16)
                act.dma_start(rows[lo:full, :], flat(src[lo * CHUNK:full * CHUNK])).then_inc(edges_in, 16)
                act.dma_start(rows[full:NCH, 0:TAIL], src[full * CHUNK:N_EDGES].unsqueeze(0)).then_inc(edges_in, 16)
            act.dma_start(b1_rows[:], b1_in.rearrange("e (j p) -> (e j) p", p=P)).then_inc(consts_in, 16)
            act.dma_start(wr[:], wr_in.rearrange("(h p) e -> p h e", p=P)).then_inc(consts_in, 16)
            act.dma_start(br[:], br_in.unsqueeze(0)).then_inc(consts_in, 16)
            act.dma_start(gamma[:], gamma_in.unsqueeze(0).to_broadcast([P, D])).then_inc(bc_in, 16)
            act.dma_start(beta[:], beta_in.unsqueeze(0).to_broadcast([P, D])).then_inc(bc_in, 16)

            def hi_part(t, b):
                act.wait_ge(tp_ready, t + 1)
                nc.scalar.activation(ht_hi[:, b, :], bank[4][:, 0:D], ACT.Copy).then_inc(hthi_ready, 1)

            def evacuate(t, b, c):
                act.wait_ge(mm_done, t * NCG + (c + 1))
                nc.scalar.activation(t_stage[:, b, c * 512:(c + 1) * 512], bank[c % 4][:], ACT.Copy
                                     ).then_inc(even_out, 1)

            act.wait_ge(w_in_sem[0], 16 * KH)
            nc.scalar.activation(w_hi[:, 0, :, :], w_raw[:, 0, :, :], ACT.Copy).then_inc(whi_ready, 1)
            hi_part(0, 0)
            for c in range(1, NCG):
                act.wait_ge(w_in_sem[c], 16 * KH)
                nc.scalar.activation(w_hi[:, c, :, :], w_raw[:, c, :, :], ACT.Copy).then_inc(whi_ready, 1)
            act.wait_ge(wlo_even, NCG // 2)
            act.wait_ge(wlo_odd, NCG // 2)

            def tile_a(t, b, last=False):
                if isinstance(t, int):
                    act.wait_ge(t_written[b], 16 * (t // 2))
                else:
                    act.wait_ge(t_written[b], t * 8 - 8 * b)
                evacuate(t, b, 0)
                evacuate(t, b, 2)
                if not last:
                    hi_part(t + 1, 1 - b)
                evacuate(t, b, 4)
                evacuate(t, b, 6)

            with act.Fori(0, NT // 2) as i:
                for b in range(2):
                    tile_a(2 * i + b, b)
            tile_a(NT - 1, 0, last=True)

            def tile_cols(b):
                return bank[b][:, 0:CT * NCH].rearrange("p (j c) -> p c j", j=CT)

            act.wait_ge(meta_tp, 1)
            nc.scalar.activation(idx_col[:], tile_cols(5), ACT.Copy).then_inc(idx_copied, 1)
            act.wait_ge(meta_tp, 2)
            nc.scalar.activation(norm_col[:], tile_cols(7), ACT.Copy).then_inc(meta_copied, 1)

            act.wait_ge(idx_copied, 1)
            with act.Fori(0, NCH // SLOTS) as i:
                for k in range(SLOTS):
                    act.wait_ge(gathered[k], i * 64)
                    nc.scalar.activation(idx_now[:, k, :], idx_col[:, bass.ds(i * SLOTS + k, 1), :].rearrange(
                        "p a b -> p (a b)"), ACT.Copy).then_inc(idx_now_ready, 1)

            act.wait_ge(b1_tp, 1)
            nc.scalar.activation(b1t[:], bank[4][:, 0:N_EXPERTS * NF], ACT.Copy).then_inc(b1t_ready, 1)

            def stage(t, s):
                act.wait_ge(acc_tp, t + 1)
                nc.scalar.activation(acc_stage[:, s, :].rearrange("p (h n) -> p h n", h=KH),
                                     acc[:, :, bass.ds(t * P, P)], ACT.Copy).then_inc(staged, 1)

            def transposed(t, j):
                act.wait_ge(xl_tp, t + 1)
                for h in range(KH):
                    nc.scalar.activation(acc[:, h, bass.ds(t * P, P)], XL_BANKS[RING[j]][:, h * P:(h + 1) * P], ACT.Copy,
                                         accum_out=mean_sum[:, h, bass.ds(t, 1)]).then_inc(xlt_ready, 1)

            act.wait_ge(acc_final, 1)
            for j in range(LG):
                stage(j, RING[j])
            with act.Fori(0, NLG - 1) as gi:
                for j in range(LG):
                    stage(gi * LG + (LG + j), RING[j])
                for j in range(LG):
                    transposed(gi * LG + j, j)
            for j in range(LG):
                transposed((NLG - 1) * LG + j, j)

            act.wait_ge(route, 3)
            nc.scalar.activation(rt[:, 2, :], rt[:, 0, :], ACT.Exp, bias=rt[:, 1, 0:1], accum_out=rt[:, 3, 0:1]
                                 ).then_inc(exp_done, 1)
            act.wait_ge(route, 10)
            nc.scalar.activation(rt[:, 8, :], rt[:, 6, :], ACT.Exp, bias=rt[:, 7, 0:1], accum_out=rt[:, 9, 0:1]
                                 ).then_inc(exp_done, 1)
            act.wait_ge(route, 14)
            nc.scalar.activation(rt[:, 13, 0:TOP_K], rt[:, 11, 0:TOP_K], ACT.Exp, bias=rt[:, 12, 0:1],
                                 accum_out=rt[:, 14, 0:1]).then_inc(exp_done, 1)
            act.wait_ge(idx_ready, 1)
            for k in range(TOP_K):
                e = act.value_load(top_i[0:1, k:k + 1], min_val=0, max_val=N_EXPERTS - 1)
                nc.scalar.activation(b1s[:, k * NF:(k + 1) * NF], b1t[:, bass.ds(e * NF, NF)], ACT.Copy
                                     ).then_inc(b1s_ready, 1)
            act.wait_ge(xl_ready, NT)
            for k in range(TOP_K):
                act.wait_ge(w1_got[k], 16)
                nc.scalar.activation(w1_hi[:, k, :, :], w1_raw[:, k, :, :], ACT.Copy).then_inc(w1hi_ready, 1)
            for k in range(TOP_K):
                act.wait_ge(w2s_ready, k + 1)
                half = slice(k * NF, k * NF + NF)
                nc.scalar.activation(w2_hi[:, half, :], w2_raw[:, half, :], ACT.Copy).then_inc(w2hi_ready, 1)
            act.wait_ge(b1s_ready, TOP_K)

            def gelu_group(gi, b):
                for u in range(NU):
                    act.wait_ge(ffn1_done, gi * NU + (u + 1))
                    act.wait_ge(glo_ready, gi * NU + (u + 1))
                    for v in range(2):
                        q = 2 * u + v
                        last = nc.scalar.activation(g[:, u % 2, v, :], bank[u][:, v * TG:(v + 1) * TG], ACT.Gelu,
                                                    bias=b1s[:, q:q + 1])
                    last.then_inc(gelu_done, 1)
                    act.wait_ge(gelu_done, gi * NU + (NU + u + 1))
                    if u == 0:
                        act.wait_ge(ffn2_done, gi * 2)
                    nc.scalar.activation(g_hi[:, b, 2 * u:2 * u + 2, :], g[:, u % 2, :, :], ACT.Copy
                                         ).then_inc(ghi_ready, 1)

            gelu_group(0, 0)
            gelu_group(1, 1)
            with act.Fori(0, 5) as i:
                gelu_group(2 * i + 2, 0)
                gelu_group(2 * i + 3, 1)
            gelu_group(12, 0)

        @block.vector
        def _(dve):
            dve.sem_inc(odd_out, 2)
            dve.sem_inc(acc_added, 2)
            dve.sem_inc(glo_ready, 2)
            dve.sem_inc(z_ready, 2)

            def stats(t, b):
                nc.vector.bn_stats(stat[:, 0, :], x[:, bass.ds(t, 1), :].rearrange("p a d -> p (a d)")
                                   ).then_inc(stat_ready, 1)
                dve.wait_ge(stat_ready, t + 1)
                nop_waits(dve)
                nc.vector.bn_aggr(mv1[:, b, :], stat[:, 0, :]).then_inc(mv_ready, 1)

            def norm(t, b):
                dve.wait_ge(rstd_ready, t + 1)
                dve.wait_ge(tp_ready, t)
                nc.vector.tensor_scalar(xn[:], x[:, bass.ds(t, 1), :].rearrange("p a d -> p (a d)"),
                                        mv1[:, b, 0:1], rstd1[:, bass.ds(t, 1)],
                                        ALU.subtract, ALU.mult).then_inc(xn_ready, 1)

            def lo_part(t, b):
                dve.wait_ge(hthi_ready, t + 1)
                nc.vector.tensor_tensor(ht_lo[:, b, :], bank[4][:, 0:D], ht_hi[:, b, :].bitcast(F32), ALU.subtract
                                        ).then_inc(htlo_ready, 1)

            def evacuate(t, b, c):
                dve.wait_ge(mm_done, t * NCG + (c + 1))
                nc.vector.tensor_copy(t_stage[:, b, c * 512:(c + 1) * 512], bank[c % 4][:]).then_inc(odd_out, 1)

            dve.wait_ge(x0_in, 16)
            stats(0, 0)
            norm(0, 0)
            for n, c in enumerate(range(0, NCG, 2)):
                dve.wait_ge(w_in_sem[c], 16 * KH)
                dve.wait_ge(whi_ready, c + 1)
                nc.vector.tensor_tensor(w_lo[:, c, :, :], w_raw[:, c, :, :], w_hi[:, c, :, :].bitcast(F32),
                                        ALU.subtract).then_inc(wlo_even, 1)
                if n == 0:
                    lo_part(0, 0)
            dve.wait_ge(x_in_sem, 48)
            dve.wait_ge(wlo_odd, NCG // 2)

            def tile_a(t, b, last=False):
                if not last:
                    stats(t + 1, 1 - b)
                if isinstance(t, int):
                    dve.wait_ge(t_written[b], 16 * (t // 2))
                else:
                    dve.wait_ge(t_written[b], t * 8 - 8 * b)
                evacuate(t, b, 1)
                if not last:
                    norm(t + 1, 1 - b)
                evacuate(t, b, 3)
                evacuate(t, b, 5)
                if not last:
                    lo_part(t + 1, 1 - b)
                evacuate(t, b, 7)

            with dve.Fori(0, NT // 2) as i:
                for b in range(2):
                    tile_a(2 * i + b, b)

            meta = [0]

            def after(ins):
                meta[0] += 1
                ins.then_inc(dve_meta, 1)
                dve.wait_ge(dve_meta, meta[0])

            dve.wait_ge(edge_math, 1)
            after(nc.vector.tensor_reduce(w0_rows[:, 0:1], dstf_rows[:], AX.X, ALU.min))
            after(nc.vector.tensor_scalar(pos_rows[:], dstf_rows[:], w0_rows[:, 0:1], None, ALU.subtract))
            after(nc.vector.tensor_scalar(srcf_rows[:], dstf_rows[:], float(NO_NODE // 2), None, ALU.is_lt))
            after(nc.vector.scalar_tensor_tensor(out=miss_rows[:], in0=pos_rows[:], scalar=float(WIN),
                                                 in1=srcf_rows[:], op0=ALU.is_ge, op1=ALU.mult))
            after(nc.vector.tensor_reduce(w0_rows[:, 1:2], miss_rows[:], AX.X, ALU.max))
            tile_a(NT - 1, 0, last=True)

            def tile_cols(b):
                return bank[b][:, 0:CT * NCH].rearrange("p (j c) -> p c j", j=CT)

            dve.wait_ge(meta_tp, 3)
            nc.vector.tensor_copy(rel_pos[:], tile_cols(6)).then_inc(meta_copied, 1)
            dve.wait_ge(meta_tp, 4)
            nc.vector.tensor_copy(dst_col[:], tile_cols(5)).then_inc(meta_copied, 1)
            dve.wait_ge(meta_tp, 5)
            nc.vector.tensor_copy(w0_row[:, 0:NCH], bank[4][0:1, 256:256 + NCH]).then_inc(meta_copied, 1)
            nc.vector.tensor_scalar(w0_row[:, NCH:NCH + 1], bank[4][0:1, 256 + NCH:257 + NCH], 0.5, None, ALU.is_gt
                                    ).then_inc(meta_copied, 1)

            dve.wait_ge(meta_copied, 5)
            dve.wait_ge(consts_ready, 2)
            dve.wait_ge(acc_zeroed, 1)
            with dve.Fori(0, NCH // SLOTS) as i:
                for k in range(SLOTS):
                    c = bass.ds(i * SLOTS + k, 1)
                    for j in range(CT):
                        last = nc.vector.tensor_scalar(sel[:, k, j, :], iota[:], rel_pos[:, c, j], norm_col[:, c, j],
                                                       ALU.is_equal, ALU.mult)
                    last.then_inc(sel_ready, 1)
                for k in range(SLOTS):
                    w0 = dve.value_load(w0_row[0:1, bass.ds(i * SLOTS + k, 1)], min_val=0, max_val=N_NODES - 1)
                    dve.wait_ge(chunk_summed, i * SLOTS + (SLOTS + k + 1))
                    dve.wait_ge(acc_added, i * SLOTS + (k + 2))
                    window = acc[:, :, bass.ds(w0, WIN)]
                    nc.vector.tensor_tensor(window, window, bank[6 + k % 2][:, 0:KH * WIN].rearrange(
                        "p (h w) -> p h w", h=KH), ALU.add).then_inc(acc_added, 1)
            dve.wait_ge(acc_added, NCH + 2)

            missed = dve.value_load(w0_row[0:1, NCH:NCH + 1], min_val=0, max_val=1)
            with dve.If(missed):
                dve.wait_ge(t_written[0], 16 * (NT // 2 + 1))
                dve.wait_ge(t_written[1], 16 * (NT // 2))
                nc.vector.tensor_copy(fb_iota[:, 0, 0:WIN], iota[:]).then_inc(fb_added, 1)
                done = 1
                dve.wait_ge(fb_added, done)
                filled = WIN
                while filled < NFB * FBW:
                    n = min(filled, NFB * FBW - filled)
                    line = fb_iota[:].rearrange("p a b -> p (a b)")
                    nc.vector.tensor_scalar(line[:, filled:filled + n], line[:, 0:n], float(filled), None, ALU.add
                                            ).then_inc(fb_added, 1)
                    done += 1
                    dve.wait_ge(fb_added, done)
                    filled += n
                nc.vector.scalar_tensor_tensor(out=fb_norm[:], in0=rel_pos[:], scalar=float(WIN), in1=norm_col[:],
                                               op0=ALU.is_ge, op1=ALU.mult).then_inc(fb_added, 1)
                done += 1
                dve.wait_ge(fb_added, done)
                with dve.Fori(0, NCH) as c:
                    with dve.Fori(0, NFB) as w:
                        s = c * NFB + w
                        for j in range(CT):
                            last = nc.vector.tensor_scalar(
                                fb_sel[:, j, :], fb_iota[:, bass.ds(w, 1), :].rearrange("p a b -> p (a b)"),
                                dst_col[:, bass.ds(c, 1), j], fb_norm[:, bass.ds(c, 1), j], ALU.is_equal, ALU.mult)
                        last.then_inc(fb_sel_ready, 1)
                        dve.wait_ge(fb_summed, s + 1)
                        for h in range(KH):
                            cols = acc[:, h, bass.ds(w * FBW, FBW)]
                            nc.vector.tensor_tensor(cols, cols, bank[6 + h][:, 0:FBW], ALU.add
                                                    ).then_inc(fb_added, 1)
                        dve.wait_ge(fb_added, s * KH + (done + KH))
            dve.drain().then_inc(acc_final, 1)

            def add_messages(t, j):
                dve.wait_ge(acc_tp, t + 1 + 2)
                tile = x[:, bass.ds(t, 1), :].rearrange("p a d -> p (a d)")
                nc.vector.tensor_tensor(tile, tile, ACC_BANKS[RING[j]][:, 0:D], ALU.add).then_inc(x1_ready, 1)
                dve.wait_ge(x1_ready, t + 1)
                nop_waits(dve)
                nc.vector.bn_stats(stat[:, j, :], tile).then_inc(stat2_ready, 1)

            def aggregate(gi):
                dve.wait_ge(stat2_ready, gi * (2 * LG) + LG)
                nop_waits(dve)
                for j in range(LG):
                    nc.vector.bn_aggr(mv2_now[:, j, :], stat[:, j, :]).then_inc(stat2_ready, 1)
                dve.wait_ge(stat2_ready, gi * (2 * LG) + 2 * LG)
                nc.vector.tensor_copy(mv2[:, bass.ds(gi * LG, LG), :], mv2_now[:]).then_inc(mv2_ready, 1)

            def normalise(gi):
                dve.wait_ge(rstd2_ready, gi + 1)
                for j in range(LG):
                    t = gi * LG + j
                    nc.vector.tensor_scalar(xn_group[:, j, :], x[:, bass.ds(t, 1), :].rearrange("p a d -> p (a d)"),
                                            mv2[:, bass.ds(t, 1), 0], rstd2[:, bass.ds(t, 1)],
                                            ALU.subtract, ALU.mult).then_inc(xng_ready, 1)

            def normalise_loop(gi):
                dve.wait_ge(xl_ready, gi * LG)
                dve.wait_ge(xl_tp, gi * LG)
                normalise(gi)

            for j in range(LG):
                add_messages(j, j)
            aggregate(0)
            with dve.Fori(0, NLG - 1) as gi:
                for j in range(LG):
                    add_messages(gi * LG + (LG + j), j)
                aggregate(gi + 1)
                normalise_loop(gi)
            normalise_loop(NLG - 1)

            n_route = [0]

            def routed(ins):
                n_route[0] += 1
                ins.then_inc(route, 1)
                dve.wait_ge(route, n_route[0])

            V = nc.vector
            dve.wait_ge(xlt_ready, KH * (NT + 2))
            V.tensor_reduce(mean[:], mean_sum[:], AX.X, ALU.add).then_inc(mean_ready, 1)
            dve.wait_ge(mean_ready, 1)
            V.tensor_scalar(mean[:], mean[:], 1.0 / N_NODES, None, ALU.mult).then_inc(mean_ready, 1)
            dve.wait_ge(logits_ready, 1)
            dve.wait_ge(consts_in, 48)
            routed(V.tensor_tensor(rt[:, 0, :], bank[5][0:1, 0:N_EXPERTS], br[:], ALU.add))
            routed(V.tensor_reduce(rt[:, 1, 1:2], rt[:, 0, :], AX.X, ALU.max))
            routed(V.tensor_scalar(rt[:, 1, 0:1], rt[:, 1, 1:2], -1.0, None, ALU.mult))
            dve.wait_ge(exp_done, 1)
            routed(V.reciprocal(rt[:, 3, 1:2], rt[:, 3, 0:1]))
            routed(V.tensor_scalar(rt[:, 4, :], rt[:, 2, :], rt[:, 3, 1:2], None, ALU.mult))
            routed(V.tensor_scalar(rt[:, 5, :], rt[:, 4, :], float(N_NODES), None, ALU.mult))
            routed(V.reciprocal(rt[:, 15, :], rt[:, 5, :]))
            routed(V.tensor_scalar(rt[:, 5, :], rt[:, 15, :], CAPACITY, 1.0, ALU.mult, ALU.min))
            routed(V.tensor_tensor(rt[:, 6, :], rt[:, 4, :], rt[:, 5, :], ALU.mult))
            V.tensor_reduce(rt[:, 7, 1:2], rt[:, 6, :], AX.X, ALU.max).then_inc(mean_ready, 1)
            dve.wait_ge(mean_ready, 3)
            routed(V.tensor_scalar(rt[:, 7, 0:1], rt[:, 7, 1:2], -1.0, None, ALU.mult))
            dve.wait_ge(exp_done, 2)
            routed(V.reciprocal(rt[:, 9, 1:2], rt[:, 9, 0:1]))
            routed(V.tensor_scalar(rt[:, 10, :], rt[:, 8, :], rt[:, 9, 1:2], None, ALU.mult))
            routed(V.max(rt[:, 11, :], rt[:, 10, :]))
            V.max_index(top_i[:], rt[:, 11, :], rt[:, 10, :]).then_inc(idx_ready, 1)
            routed(V.tensor_scalar(rt[:, 12, 0:1], rt[:, 11, 0:1], -1.0, None, ALU.mult))
            dve.wait_ge(exp_done, 3)
            routed(V.reciprocal(rt[:, 14, 1:2], rt[:, 14, 0:1]))
            dve.wait_ge(consts_ready, 1)
            for k in range(TOP_K):
                routed(V.tensor_scalar(rt[:, 15, k:k + 1], rt[:, 13, k:k + 1], rt[:, 14, 1:2], None, ALU.mult))
            for k in range(TOP_K):
                V.tensor_scalar(w_rows[:, k, :], ones[0:1, :], rt[:, 15, k:k + 1], None, ALU.mult).then_inc(wts_ready, 1)

            def w1_lo_part(k):
                dve.wait_ge(w1hi_ready, k + 1)
                V.tensor_tensor(w1_lo[:, k, :, :], w1_raw[:, k, :, :], w1_hi[:, k, :, :].bitcast(F32), ALU.subtract
                                ).then_inc(w1lo_ready, 1)

            def token_lo(gi, b):
                dve.wait_ge(xshi_ready, gi + 1)
                V.tensor_tensor(xs_lo[:, b, :, :], acc[:, :, bass.ds(gi * TG, TG)], xs_hi[:, b, :, :].bitcast(F32),
                                ALU.subtract).then_inc(xslo_ready, 1)

            token_lo(0, 0)
            token_lo(1, 1)
            w1_lo_part(0)
            dve.wait_ge(wcol_ps, 1)
            V.tensor_copy(w_cols[:], bank[5][:, 16:16 + TOP_K]).then_inc(wcol_ready, 1)
            dve.wait_ge(wcol_ready, 1)
            for k in range(TOP_K):
                dve.wait_ge(w2_got[k], 16)
                half = w2_raw[:, k * NF:(k + 1) * NF, :]
                V.tensor_scalar(half, half, w_cols[:, k:k + 1], None, ALU.mult).then_inc(w2s_ready, 1)
                if k == 0:
                    w1_lo_part(1)
            dve.wait_ge(b2_ps, 1)
            V.tensor_copy(b2c[:], bank[6][:, 0:D]).then_inc(b2_ready, 1)

            def gelu_lo(gi, b, u):
                dve.wait_ge(ghi_ready, gi * NU + (u + 1))
                V.tensor_tensor(g_lo[:, b, 2 * u:2 * u + 2, :], g[:, u % 2, :, :],
                                g_hi[:, b, 2 * u:2 * u + 2, :].bitcast(F32), ALU.subtract).then_inc(glo_ready, 1)

            def residual(gi, b, n):
                if not isinstance(gi, int) or gi >= 2:
                    dve.wait_ge(o_ready, gi - 1)
                dve.wait_ge(xlb_ready, gi + 1)
                for s in range(n):
                    dve.wait_ge(ffn2_done, gi * 2 + (s + 1 + 2))
                    V.tensor_tensor(z[:, b, s, :], bank[4 + s][:, 0:D],
                                    xl[:, bass.ds(gi * 2 + s, 1), :].rearrange("p a d -> p (a d)"), ALU.add
                                    ).then_inc(z_ready, 1)
                for s in range(n):
                    dve.wait_ge(z_ready, gi * 2 + (s + 1 + 2))
                    V.bn_stats(stat[:, s, :], z[:, b, s, :]).then_inc(stat3_ready, 1)
                dve.wait_ge(stat3_ready, gi * 2 + n)
                nop_waits(dve)
                for s in range(n):
                    last = V.bn_aggr(mv3[:, b, s, :], stat[:, s, :])
                last.then_inc(mv3_ready, 1)

            def norm_out(gi, b, n):
                dve.wait_ge(rstd3_ready, gi + 1)
                for s in range(n):
                    last = V.tensor_scalar(z[:, b, s, :], z[:, b, s, :], mv3[:, b, s, 0:1],
                                           rstd3[:, bass.ds(gi * 2 + s, 1)], ALU.subtract, ALU.mult)
                last.then_inc(zn_ready, 1)

            for u in range(NU):
                gelu_lo(0, 0, u)

            def step(gi, b, first=False):
                if not isinstance(gi, int) or gi + 1 < NG:
                    gelu_lo(gi + 1, 1 - b, 0)
                    gelu_lo(gi + 1, 1 - b, 1)
                if not first:
                    norm_out(gi - 1, 1 - b, 2)
                if not isinstance(gi, int) or gi + 1 < NG:
                    gelu_lo(gi + 1, 1 - b, 2)
                    gelu_lo(gi + 1, 1 - b, 3)
                if not isinstance(gi, int) or gi + 2 < NG:
                    token_lo(gi + 2, b)
                residual(gi, b, 1 if isinstance(gi, int) and gi == NG - 1 else 2)

            step(0, 0, first=True)
            with dve.Fori(0, 5) as i:
                step(2 * i + 1, 1)
                step(2 * i + 2, 0)
            step(11, 1)
            step(12, 0)
            norm_out(12, 0, 1)

        @block.tensor
        def _(pe):
            pe.sem_inc(chunk_summed, SLOTS)
            pe.sem_inc(acc_tp, 2)
            pe.sem_inc(ffn2_done, 2)
            mm = nc.tensor.matmul

            def split_product(out_ap, a_hi, a_lo, b_hi, b_lo, first, last):
                mm(out_ap, a_lo, b_hi, start=first, stop=False)
                mm(out_ap, a_hi, b_lo, start=False, stop=False)
                return mm(out_ap, a_hi, b_hi, start=False, stop=last)

            def transposes(t, ready, src, bank_ap, done):
                pe.wait_ge(ready, t + 1)
                for h in range(KH):
                    last = nc.tensor.transpose(bank_ap[:, h * P:(h + 1) * P], src[:, h * P:(h + 1) * P], ident[:])
                last.then_inc(done, 1)

            def tile_a(t, b, last=False):
                pe.wait_ge(htlo_ready, t + 1)
                for c in range(NCG):
                    if c == NCG // 2 and not last:
                        transposes(t + 1, xn_ready, xn, bank[4], tp_ready)
                    pe.wait_ge(wlo_even if c % 2 == 0 else wlo_odd, c // 2 + 1)
                    pe.wait_ge(even_out if c % 2 == 0 else odd_out, t * (NCG // 2) + (c // 2 + 1))
                    for kh in range(KH):
                        rows = slice(kh * P, (kh + 1) * P)
                        done = split_product(bank[c % 4][:], ht_hi[:, b, rows], ht_lo[:, b, rows],
                                             w_hi[:, c, kh, :], w_lo[:, c, kh, :], kh == 0, kh == KH - 1)
                    done.then_inc(mm_done, 1)

            pe.wait_ge(ident_ready, 1)
            transposes(0, xn_ready, xn, bank[4], tp_ready)
            with pe.Fori(0, NT // 2) as i:
                for b in range(2):
                    tile_a(2 * i + b, b)
            tile_a(NT - 1, 0, last=True)

            def to_columns(rows, b, done):
                for j in range(CT):
                    last = nc.tensor.transpose(bank[b][:, j * NCH:(j + 1) * NCH], rows[:, j * P:(j + 1) * P],
                                               ident[0:NCH, 0:NCH])
                last.then_inc(done, 1)

            pe.wait_ge(edge_math, 1)
            to_columns(idxf_rows, 5, meta_tp)
            to_columns(norm_rows, 7, meta_tp)
            pe.wait_ge(dve_meta, 5)
            to_columns(pos_rows, 6, meta_tp)
            pe.wait_ge(idx_copied, 1)
            to_columns(dstf_rows, 5, meta_tp)
            pe.wait_ge(consts_ready, 1)
            mm(bank[4][0:1, 256:256 + NCH], w0_rows[:, 0:1], ident[0:NCH, 0:NCH], start=True, stop=True)
            mm(bank[4][0:1, 256 + NCH:257 + NCH], w0_rows[:, 1:2], ones[0:NCH, 0:1], start=True, stop=True
               ).then_inc(meta_tp, 1)

            pe.wait_ge(meta_copied, 5)
            pe.wait_ge(consts_in, 48)
            nc.tensor.transpose(bank[4][:, 0:N_EXPERTS * NF], b1_rows[:],
                                ident[0:N_EXPERTS * NF, 0:N_EXPERTS * NF]).then_inc(b1_tp, 1)
            with pe.Fori(0, NCH // SLOTS) as i:
                for k in range(SLOTS):
                    pe.wait_ge(sel_ready, i * SLOTS + (k + 1))
                    pe.wait_ge(acc_added, i * SLOTS + (k + 1))
                    pe.wait_ge(gathered[k], i * 64 + 64)
                    for h in range(KH):
                        for j in range(CT):
                            last = mm(bank[6 + k % 2][:, h * WIN:(h + 1) * WIN], gath[:, k, j, h * P:(h + 1) * P],
                                      sel[:, k, j, :], start=j == 0, stop=j == CT - 1)
                    last.then_inc(chunk_summed, 1)

            missed = pe.value_load(w0_row[0:1, NCH:NCH + 1], min_val=0, max_val=1)
            with pe.If(missed):
                pe.wait_ge(acc_added, NCH + 2)
                with pe.Fori(0, NCH) as c:
                    with pe.Fori(0, NFB) as w:
                        pe.wait_ge(fb_gathered, c * 64 + 64)
                        pe.wait_ge(fb_sel_ready, c * NFB + w + 1)
                        for h in range(KH):
                            for j in range(CT):
                                last = mm(bank[6 + h][:, 0:FBW], gath[:, 0, j, h * P:(h + 1) * P], fb_sel[:, j, :],
                                          start=j == 0, stop=j == CT - 1)
                        last.then_inc(fb_summed, 1)

            def acc_tile(t, j):
                if not isinstance(t, int) or t >= 2:
                    pe.wait_ge(x1_ready, t - 1)
                transposes(t, staged, acc_stage[:, RING[j], :], ACC_BANKS[RING[j]], acc_tp)

            def xl_tile(t, j):
                pe.wait_ge(xlt_ready, t * KH + KH)
                transposes(t, xng_ready, xn_group[:, j, :], XL_BANKS[RING[j]], xl_tp)

            for j in range(LG):
                acc_tile(j, j)
            with pe.Fori(0, NLG - 1) as gi:
                for j in range(LG):
                    acc_tile(gi * LG + (LG + j), j)
                for j in range(LG):
                    xl_tile(gi * LG + j, j)
            for j in range(LG):
                xl_tile((NLG - 1) * LG + j, j)

            pe.wait_ge(mean_ready, 2)
            pe.wait_ge(b1t_ready, 1)
            for h in range(KH):
                last = mm(bank[5][0:1, 0:N_EXPERTS], mean[:, h:h + 1], wr[:, h, :], start=h == 0, stop=h == KH - 1)
            last.then_inc(logits_ready, 1)
            pe.wait_ge(wts_ready, TOP_K)
            mm(bank[5][:, 16:16 + TOP_K], ones[0:1, :], rt[:, 15, 0:TOP_K], start=True, stop=True).then_inc(wcol_ps, 1)
            pe.wait_ge(b2_got, 16 * TOP_K)
            for k in range(TOP_K):
                last = mm(bank[6][:, 0:D], w_rows[:, k, :], b2_pair[:, k, :], start=k == 0, stop=k == TOP_K - 1)
            last.then_inc(b2_ps, 1)

            def ffn1(gi, b):
                pe.wait_ge(xslo_ready, gi + 1)
                for u in range(NU):
                    if isinstance(gi, int) and gi == 0:
                        pe.wait_ge(w1lo_ready, u // (NU // TOP_K) + 1)
                    pe.wait_ge(gelu_done, gi * NU + (u + 1))
                    for v in range(2):
                        k, f = divmod(2 * u + v, NF)
                        for kh in range(KH):
                            cols = slice(f * P, (f + 1) * P)
                            last = split_product(bank[u][:, v * TG:(v + 1) * TG], w1_hi[:, k, kh, cols],
                                                 w1_lo[:, k, kh, cols], xs_hi[:, b, kh, :], xs_lo[:, b, kh, :],
                                                 kh == 0, kh == KH - 1)
                    last.then_inc(ffn1_done, 1)

            def ffn2(gi, b, n):
                pe.wait_ge(glo_ready, gi * NU + (NU + 2))
                for s in range(n):
                    pe.wait_ge(z_ready, gi * 2 + (s + 1))
                    for q in range(NQ):
                        rows = slice(s * P, (s + 1) * P)
                        last = split_product(bank[4 + s][:, 0:D], g_hi[:, b, q, rows], g_lo[:, b, q, rows],
                                             w2_hi[:, q, :], w2_lo[:, q, :], q == 0, q == NQ - 1)
                    last.then_inc(ffn2_done, 1)

            ffn1(0, 0)
            ffn1(1, 1)
            pe.wait_ge(w2lo_ready, TOP_K)
            pe.wait_ge(b2_ready, 1)
            ffn2(0, 0, 2)
            with pe.Fori(0, 5) as i:
                ffn1(2 * i + 2, 0)
                ffn2(2 * i + 1, 1, 2)
                ffn1(2 * i + 3, 1)
                ffn2(2 * i + 2, 0, 2)
            ffn1(12, 0)
            ffn2(11, 1, 2)
            ffn2(12, 0, 1)


_INS = ['x', 'src', 'dst', 'edge_type_16', 'edge_weight1', 'L0_gnn_weight', 'L0_ffn_Wr', 'L0_ffn_br', 'L0_ffn_W1',
        'L0_ffn_b1', 'L0_ffn_W2', 'L0_ffn_b2', 'L0_ffn_gamma', 'L0_ffn_beta']


def build(nc, shapes):
    args = [nc.dram_tensor(f"in_{n}_dram", s, d, kind="ExternalInput").ap() for n, (s, d) in shapes.items()]
    args.append(nc.dram_tensor("out_0_dram", (N_NODES, D), F32, kind="ExternalOutput").ap())
    gnn_ffn(nc, *args)


def kernel(**inputs):
    import concourse.bacc as _bacc
    from concourse.bass_utils import run_bass_kernel_spmd as _run

    nc = _bacc.Bacc("TRN2", target_bir_lowering=False, num_devices=1)
    arrays = {f"in_{n}_dram": np.ascontiguousarray(inputs[n]) for n in _INS}
    build(nc, {n: (arrays[f"in_{n}_dram"].shape, mybir.dt.from_np(arrays[f"in_{n}_dram"].dtype)) for n in _INS})
    r = _run(nc, [arrays], core_ids=[0])
    return r.results[0]["out_0_dram"]
```

```python
import numpy as np
import concourse.bass as bass
from concourse import mybir
from contextlib import ExitStack

F32 = mybir.dt.float32
F32R = mybir.dt.float32r
I32 = mybir.dt.int32
U32 = mybir.dt.uint32
ALU = mybir.AluOpType
ACT = mybir.ActivationFunctionType
AX = mybir.AxisListType

P = 128
N_NODES, D = 3125, 256
N_RELS = 16
N_EDGES = 53125
N_EXPERTS, D_FF, TOP_K = 8, 512, 2
LN_EPS = 1e-5
CAPACITY = float(-(-N_NODES * 5 // (4 * N_EXPERTS)))

KH = D // P
NT = -(-N_NODES // P)
LAST = N_NODES - (NT - 1) * P
TROW = N_RELS * D
NCG = TROW // 512

CHUNK = 512
NCH = -(-N_EDGES // CHUNK)
CT = CHUNK // P
TAIL = N_EDGES - (NCH - 1) * CHUNK
SLOTS = 4
WIN = 64
NO_NODE = 1 << 20
FBW = 400
NFB = -(-NT * P // FBW)
NIT = NCH // SLOTS
LAG = 3

TG = 2 * P
NG = -(-NT * P // TG)
NF = D_FF // P
NQ = TOP_K * NF
NU = NQ // 2
ACOLS = NG * TG
LG = 5
NLG = NT // LG
NEWTON = 11
assert NT % 2 == 1 and NT == NLG * LG and NCH % SLOTS == 0 and NG == 13


def gnn_ffn(nc, x_in, src_in, dst_in, rel_in, norm_in, w_in, wr_in, br_in, w1_in, b1_in, w2_in, b2_in,
            gamma_in, beta_in, out):
    table = nc.dram_tensor("table", [NT * P * N_RELS, D], F32, kind="Internal").ap()
    table_tiles = table.rearrange("(t p r) d -> t p (r d)", p=P, r=N_RELS)

    ctx = ExitStack()
    with ctx:
        base = [16512]

        def region(nbytes):
            at = base[0]
            base[0] = at + -(-nbytes // 32) * 32
            assert base[0] <= nc.sbuf_usable_end, base[0]
            return at

        def at(name, shape, dtype, offset):
            return nc.alloc_sbuf_tensor_at(name, shape, dtype, offset=offset)

        def sb(name, shape, dtype=F32):
            return at(name, shape, dtype, region(4 * int(np.prod(shape[1:]))))

        def sem(name):
            return ctx.enter_context(nc.semaphore(name))

        x = sb("x", [P, NT, D])
        acc = sb("acc", [P, KH, ACOLS])
        ident = sb("ident", [P, P])
        minus_half = sb("minus_half", [P, LG])
        eps = sb("eps", [P, LG])
        gamma = sb("gamma", [P, D])
        beta = sb("beta", [P, D])
        wr = sb("wr", [P, KH, N_EXPERTS])
        b1t = sb("b1t", [P, N_EXPERTS * NF])
        b1s = sb("b1s", [P, NQ])
        stat = sb("stat", [P, LG, 6])
        mv1 = sb("mv1", [P, 2, 2])
        var_eps = sb("var_eps", [P, LG])
        rstd1 = sb("rstd1", [P, NT])
        mv2 = sb("mv2", [P, 2])
        root = sb("root", [P, 3])
        thr_i = sb("thr_i", [NCH, 2], I32)
        thr = sb("thr", [NCH, 2])
        mv3 = sb("mv3", [P, 2, 2, 2])
        rstd3 = sb("rstd3", [P, 2 * NG])
        iota_i = sb("iota_i", [P, WIN], I32)
        iota = sb("iota", [P, WIN])
        idx_col = sb("idx_col", [P, NCH, CT], I32)
        norm_col = sb("norm_col", [P, NCH, CT])
        idx_now = sb("idx_now", [P, SLOTS, CT], I32)
        w0_row = sb("w0_row", [1, NCH + 1], I32)
        xn = sb("xn", [P, D])
        ht_hi = sb("ht_hi", [P, 2, D], F32R)
        ht_lo = sb("ht_lo", [P, 2, D], F32R)
        acc_stage = sb("acc_stage", [P, D])
        xs_hi = sb("xs_hi", [P, 2, KH, TG], F32R)
        xs_lo = sb("xs_lo", [P, 2, KH, TG], F32R)
        g = sb("g", [P, 2, 2, TG])

        r_big = region(65536)
        w_hi = at("w_hi", [P, NCG, KH, 512], F32R, r_big)
        w_lo = at("w_lo", [P, NCG, KH, 512], F32R, r_big + 32768)
        w1_hi = at("w1_hi", [P, TOP_K, KH, D_FF], F32R, r_big)
        w1_lo = at("w1_lo", [P, TOP_K, KH, D_FF], F32R, r_big + 8192)
        w2_hi = at("w2_hi", [P, NQ, D], F32R, r_big + 16384)
        w2_lo = at("w2_lo", [P, NQ, D], F32R, r_big + 24576)
        g_hi = at("g_hi", [P, 2, NQ, TG], F32R, r_big + 32768)
        g_lo = at("g_lo", [P, 2, NQ, TG], F32R, r_big + 49152)
        r_cols = region(4096)
        rel_pos = at("rel_pos", [P, NCH, CT], F32, r_cols)
        dst_col = at("dst_col", [P, NCH, CT], F32, r_cols + 1664)
        z = at("z", [P, 2, 2, D], F32, r_cols)
        r_sel = region(4096)
        sel = at("sel", [P, SLOTS, CT, WIN], F32, r_sel)
        o = at("o", [P, 2, 2, D], F32, r_sel)
        r_stage = region(32768)
        w_raw = at("w_raw", [P, NCG, KH, 512], F32, r_stage)
        t_stage = at("t_stage", [P, 2, TROW], F32, r_stage)
        xl = at("xl", [P, 2 * NG, D], F32, r_stage)
        fb_iota = at("fb_iota", [P, NFB, FBW], F32, r_stage + 1600)
        fb_sel = at("fb_sel", [P, CT, FBW], F32, r_stage + 1600 + 12800)
        fb_norm = at("fb_norm", [P, NCH, CT], F32, r_stage + 1600 + 12800 + 6400)
        r_gather = region(16384)
        gath = at("gath", [P, SLOTS, CT, D], F32, r_gather)
        src_rows = at("src_rows", [NCH, CHUNK], I32, r_gather)
        rel_rows = at("rel_rows", [NCH, CHUNK], I32, r_gather + 2048)
        dst_rows = at("dst_rows", [NCH, CHUNK], I32, r_gather + 4096)
        norm_rows = at("norm_rows", [NCH, CHUNK], F32, r_gather + 6144)
        srcf_rows = at("srcf_rows", [NCH, CHUNK], F32, r_gather + 8192)
        idxf_rows = at("idxf_rows", [NCH, CHUNK], F32, r_gather + 10240)
        dstf_rows = at("dstf_rows", [NCH, CHUNK], F32, r_gather + 12288)
        relf_rows = at("relf_rows", [NCH, CHUNK], F32, r_gather + 14336)
        w1_raw = at("w1_raw", [P, TOP_K, KH, D_FF], F32, r_gather)
        w2_raw = at("w2_raw", [P, NQ, D], F32, r_gather + 8192)
        b1_rows = sb("b1_rows", [N_EXPERTS * NF, P])
        w0_rows = sb("w0_rows", [NCH, 2])
        ones = sb("ones", [P, P])
        mean_sum = sb("mean_sum", [P, KH, NT])
        mean = sb("mean", [P, KH])
        rt = sb("rt", [1, 16, N_EXPERTS])
        top_i = sb("top_i", [1, 8], U32)
        b2_pair = sb("b2_pair", [1, TOP_K, D])
        w_rows = sb("w_rows", [1, TOP_K, P])
        w_cols = sb("w_cols", [P, TOP_K])
        b2c = sb("b2c", [P, D])
        br = sb("br", [1, N_EXPERTS])

        pos_rows = at("pos_rows", [NCH, CHUNK], F32, r_gather + 2048)
        miss_rows = at("miss_rows", [NCH, CHUNK], F32, r_gather)

        bank = [ctx.enter_context(nc.psum_tensor(f"bank{i}", [P, 512], F32)) for i in range(8)]

        x0_in, x12_in, x_in_sem, edges_in, consts_in = sem("x0_in"), sem("x12_in"), sem("x_in"), sem("edges_in"), sem("consts_in")
        bc_in = sem("bc_in")
        w_in_sem = [sem(f"w_in{c}") for c in range(NCG)]
        x_zeroed, rows_filled, ident_ready = sem("x_zeroed"), sem("rows_filled"), sem("ident_ready")
        pool_step = sem("pool_step")
        consts_ready = sem("consts_ready")
        whi_ready, wlo_even, wlo_odd = sem("whi_ready"), sem("wlo_even"), sem("wlo_odd")
        stat_ready, mv_ready, rstd_ready, xn_ready = sem("stat_ready"), sem("mv_ready"), sem("rstd_ready"), sem("xn_ready")
        tp_ready, hthi_ready, htlo_ready = sem("tp_ready"), sem("hthi_ready"), sem("htlo_ready")
        mm_done, even_out, odd_out = sem("mm_done"), sem("even_out"), sem("odd_out")
        t_written = [sem("t_written0"), sem("t_written1")]
        edge_math, dve_meta, meta_tp, meta_copied = sem("edge_math"), sem("dve_meta"), sem("meta_tp"), sem("meta_copied")
        idx_copied, acc_zeroed = sem("idx_copied"), sem("acc_zeroed")
        idx_now_ready = sem("idx_now_ready")
        gathered = [sem(f"gathered{k}") for k in range(SLOTS)]
        sel_ready, chunk_summed, acc_added = sem("sel_ready"), sem("chunk_summed"), sem("acc_added")
        fb_step, fb_sel_ready, fb_summed, fb_added, fb_gathered = (
            sem("fb_step"), sem("fb_sel_ready"), sem("fb_summed"), sem("fb_added"), sem("fb_gathered"))
        acc_final = sem("acc_final")
        newton = sem("newton")
        xn2_ready = sem("xn2_ready")
        staged, acc_tp, x1_ready = sem("staged"), sem("acc_tp"), sem("x1_ready")
        stat2_ready, mv2_ready, rstd2_ready = sem("stat2_ready"), sem("mv2_ready"), sem("rstd2_ready")
        xng_ready, xl_tp, xlt_ready, xl_ready = sem("xng_ready"), sem("xl_tp"), sem("xlt_ready"), sem("xl_ready")
        mean_ready, logits_ready, route, exp_done = sem("mean_ready"), sem("logits_ready"), sem("route"), sem("exp_done")
        idx_ready = sem("idx_ready")
        w1_got = [sem(f"w1_got{e}") for e in range(TOP_K)]
        w2_got = [sem(f"w2_got{e}") for e in range(TOP_K)]
        b2_got = sem("b2_got")
        wts_ready, wcol_ps, wcol_ready, b2_ps, b2_ready = (
            sem("wts_ready"), sem("wcol_ps"), sem("wcol_ready"), sem("b2_ps"), sem("b2_ready"))
        b1_tp, b1t_ready, b1s_ready = sem("b1_tp"), sem("b1t_ready"), sem("b1s_ready")
        w1hi_ready, w1lo_ready, w2s_ready, w2hi_ready, w2lo_ready = (
            sem("w1hi_ready"), sem("w1lo_ready"), sem("w2s_ready"), sem("w2hi_ready"), sem("w2lo_ready"))
        xshi_ready, xslo_ready = sem("xshi_ready"), sem("xslo_ready")
        ffn1_done, gelu_done, ghi_ready, glo_ready = sem("ffn1_done"), sem("gelu_done"), sem("ghi_ready"), sem("glo_ready")
        ffn2_done, xlb_ready, z_ready, stat3_ready, mv3_ready = (
            sem("ffn2_done"), sem("xlb_ready"), sem("z_ready"), sem("stat3_ready"), sem("mv3_ready"))
        rstd3_ready, zn_ready, o_ready = sem("rstd3_ready"), sem("zn_ready"), sem("o_ready")
        fin_step = sem("fin_step")
        out_written = [sem("out_written0"), sem("out_written1")]

        block = ctx.enter_context(nc.Block())

        def nop_waits(engine):
            engine.nop(nofuse=True)

        def flat(a):
            return a.rearrange("(c e) -> c e", e=CHUNK)

        @block.sync
        def _(sp):
            sp.dma_start(x[:, 0, :], x_in[0:P, :]).then_inc(x0_in, 16)
            for c in range(NCG):
                if c == NCG // 2:
                    sp.dma_start(x[:, 1:3, :], x_in[P:3 * P, :].rearrange("(t p) d -> p t d", p=P)).then_inc(x12_in, 16)
                for kh in range(KH):
                    sp.dma_start(w_raw[:, c, kh, :].rearrange("p (r o) -> p r o", r=2),
                                 w_in[2 * c:2 * c + 2, kh * P:(kh + 1) * P, :].rearrange("r p o -> p r o")
                                 ).then_inc(w_in_sem[c], 16)
            sp.wait_ge(w_in_sem[NCG - 1], 16 * KH)
            sp.dma_start(x[:, 3:NT - 1, :],
                         x_in[3 * P:(NT - 1) * P, :].rearrange("(t p) d -> p t d", p=P)).then_inc(x_in_sem, 16)
            sp.wait_ge(x_zeroed, 1)
            full = LAST // 16 * 16
            sp.dma_start(x[0:full, NT - 1, :], x_in[(NT - 1) * P:(NT - 1) * P + full, :]).then_inc(x_in_sem, 16)
            sp.dma_start(x[full:LAST, NT - 1, :], x_in[(NT - 1) * P + full:N_NODES, :]).then_inc(x_in_sem, 16)
            def store_table(t, b):
                sp.wait_ge(even_out, NCG // 2 * (t + 1) + 2)
                sp.wait_ge(odd_out, NCG // 2 * (t + 1) + 2)
                sp.dma_start(table_tiles[t], t_stage[:, b, :]).then_inc(t_written[b], 16)

            def store_table_in_parts(t, b):
                for n in range(NCG // 2):
                    sp.wait_ge(even_out, NCG // 2 * t + n + 3)
                    sp.wait_ge(odd_out, NCG // 2 * t + n + 3)
                    part = slice(n * 1024, (n + 1) * 1024)
                    sp.dma_start(table_tiles[t][:, part], t_stage[:, b, part]).then_inc(t_written[b], 16)

            with sp.Fori(0, NT // 2) as i:
                for b in range(2):
                    store_table(2 * i + b, b)
            store_table_in_parts(NT - 1, 0)

            sp.wait_ge(idx_ready, 1)
            for k in range(TOP_K):
                e = sp.value_load(top_i[0:1, k:k + 1], min_val=0, max_val=N_EXPERTS - 1)
                sp.dma_start(w1_raw[:, k, :, :], w1_in.rearrange("e (h p) f -> e p h f", p=P)[e]
                             ).then_inc(w1_got[k], 16)
                sp.dma_start(w2_raw[:, k * NF:(k + 1) * NF, :], w2_in.rearrange("e (j p) d -> e p j d", p=P)[e]
                             ).then_inc(w2_got[k], 16)
                sp.dma_start(b2_pair[0:1, k, :], b2_in[bass.ds(e, 1), :]).then_inc(b2_got, 16)

            def store_out(gi, b, full_group):
                sp.wait_ge(o_ready, gi + 1)
                if full_group:
                    sp.dma_start(out[bass.ds(gi * TG, TG), :].rearrange("(s p) d -> p s d", p=P),
                                 o[:, b, :, :]).then_inc(out_written[b], 16)
                else:
                    sp.dma_start(out[gi * TG:gi * TG + full, :], o[0:full, b, 0, :]).then_inc(out_written[b], 16)
                    sp.dma_start(out[gi * TG + full:N_NODES, :], o[full:LAST, b, 0, :]).then_inc(out_written[b], 16)

            with sp.Fori(0, NG // 2) as i:
                for b in range(2):
                    store_out(2 * i + b, b, True)
            store_out(NG - 1, 0, False)
            sp.wait_ge(out_written[0], 16 * (NG // 2) + 32)
            sp.wait_ge(out_written[1], 16 * (NG // 2))

        @block.gpsimd
        def _(pool):
            steps = [0]

            def after(ins):
                steps[0] += 1
                ins.then_inc(pool_step, 1)
                pool.wait_ge(pool_step, steps[0])

            nc.gpsimd.memset(x[:, NT - 1, :], 0.0).then_inc(x_zeroed, 1)
            pool.wait_ge(x_zeroed, 1)
            lo = NCH // 32 * 32
            nc.gpsimd.memset(src_rows[lo:NCH, :], 0).then_inc(rows_filled, 1)
            nc.gpsimd.memset(rel_rows[lo:NCH, :], 0).then_inc(rows_filled, 1)
            nc.gpsimd.memset(norm_rows[lo:NCH, :], 0.0).then_inc(rows_filled, 1)
            nc.gpsimd.memset(dst_rows[lo:NCH, :], NO_NODE).then_inc(rows_filled, 1)
            pool.wait_ge(rows_filled, 4)
            after(nc.gpsimd.memset(ident[:], 0.0))
            nc.gpsimd.affine_select(out=ident[:], in_=ident[:], compare_op=ALU.not_equal, fill=1.0, base=0,
                                    pattern=[[-1, P]], channel_multiplier=1).then_inc(ident_ready, 1)
            after(nc.gpsimd.memset(minus_half[:], -0.5))
            after(nc.gpsimd.memset(eps[:], LN_EPS))

            def rstd_pool(var, out_ap, n, half, ready, step_at):
                nc.gpsimd.tensor_tensor(var_eps[:, 0:n], var, eps[:, 0:n], ALU.add).then_inc(pool_step, 1)
                pool.wait_ge(pool_step, step_at)
                nc.gpsimd.tensor_tensor(out_ap, var_eps[:, 0:n], half, ALU.pow).then_inc(ready, 1)

            pool.wait_ge(mv_ready, 1)
            steps[0] += 1
            rstd_pool(mv1[:, 0, 1:2], rstd1[:, 0:1], 1, minus_half[:, 0:1], rstd_ready, steps[0])
            for c in range(1, NCG, 2):
                pool.wait_ge(w_in_sem[c], 16 * KH)
                pool.wait_ge(whi_ready, c + 1)
                nc.gpsimd.tensor_tensor(w_lo[:, c, :, :], w_raw[:, c, :, :], w_hi[:, c, :, :].bitcast(F32),
                                        ALU.subtract).then_inc(wlo_odd, 1)
            pool.wait_ge(mv_ready, 2)
            pool.wait_ge(rstd_ready, 1)
            steps[0] += 1
            rstd_pool(mv1[:, 1, 1:2], rstd1[:, 1:2], 1, minus_half[:, 0:1], rstd_ready, steps[0])
            nc.gpsimd.memset(ones[:], 1.0)
            nc.gpsimd.iota(thr_i[:, 0:1], [[0, 1]], base=0, channel_multiplier=1)
            nc.gpsimd.iota(iota_i[:], [[1, WIN]], base=0, channel_multiplier=0).then_inc(consts_ready, 1)
            pool.wait_ge(consts_ready, 1)
            nc.gpsimd.tensor_copy(iota[:], iota_i[:]).then_inc(consts_ready, 1)
            base_steps = steps[0]

            def rstd_tile(t, b):
                pool.wait_ge(mv_ready, t + 1)
                pool.wait_ge(rstd_ready, t)
                rstd_pool(mv1[:, b, 1:2], rstd1[:, bass.ds(t, 1)], 1, minus_half[:, 0:1], rstd_ready,
                          t + (base_steps - 1))

            with pool.Fori(0, (NT - 3) // 2) as i:
                rstd_tile(2 * i + 2, 0)
                rstd_tile(2 * i + 3, 1)
            rstd_tile(NT - 1, 0)
            steps[0] = base_steps + (NT - 2)
            nc.gpsimd.memset(acc[:], 0.0).then_inc(acc_zeroed, 1)
            pool.wait_ge(edges_in, 4 * 3 * 16)
            nc.gpsimd.tensor_copy(srcf_rows[:], src_rows[:])
            nc.gpsimd.tensor_copy(relf_rows[:], rel_rows[:])
            after(nc.gpsimd.tensor_copy(dstf_rows[:], dst_rows[:]))
            after(nc.gpsimd.tensor_scalar(idxf_rows[:], srcf_rows[:], float(N_RELS), 0.0, ALU.mult, ALU.add))
            nc.gpsimd.tensor_tensor(idxf_rows[:], idxf_rows[:], relf_rows[:], ALU.add).then_inc(edge_math, 1)

            pool.wait_ge(t_written[0], 16 * (NT // 2 + NCG // 2))
            pool.wait_ge(t_written[1], 16 * (NT // 2))
            pool.wait_ge(meta_tp, 4)

            def gather(slot, signal):
                nop_waits(pool)
                for j in range(CT):
                    nc.gpsimd.indirect_dma_start(
                        out=gath[:, slot, j, :], out_offset=None, in_=table,
                        in_offset=bass.IndirectOffsetOnAxis(ap=idx_now[:, slot, j:j + 1], axis=0)
                    ).then_inc(signal, 16)

            with pool.Fori(0, NCH // SLOTS) as i:
                for k in range(SLOTS):
                    pool.wait_ge(idx_now_ready, i * SLOTS + k + 1)
                    pool.wait_ge(chunk_summed, i * SLOTS + k + 1)
                    gather(k, gathered[k])

            pool.wait_ge(meta_copied, 5)
            for k in range(SLOTS):
                pool.wait_ge(gathered[k], 64 * (NCH // SLOTS))
            pool.wait_ge(chunk_summed, NCH + SLOTS)
            missed = pool.value_load(w0_row[0:1, NCH:NCH + 1], min_val=0, max_val=1)
            with pool.If(missed):
                with pool.Fori(0, NCH) as c:
                    pool.wait_ge(fb_summed, c * NFB)
                    nc.gpsimd.tensor_copy(idx_now[:, 0, :], idx_col[:, bass.ds(c, 1), :].rearrange("p a b -> p (a b)")
                                          ).then_inc(fb_step, 1)
                    pool.wait_ge(fb_step, c + 1)
                    gather(0, fb_gathered)
                    pool.wait_ge(fb_gathered, c * 64 + 64)

            def add_b2(gi, n):
                cols = xl[:, bass.ds(gi * 2, n), :]
                nc.gpsimd.tensor_tensor(cols, cols, b2c[:].unsqueeze(1).to_broadcast([P, n, D]), ALU.add
                                        ).then_inc(xlb_ready, 1)

            def rstd_out(gi, b, n, step_at):
                pool.wait_ge(mv3_ready, gi + 1)
                rstd_pool(mv3[:, b, 0:n, 1], rstd3[:, bass.ds(gi * 2, n)], n, minus_half[:, 0:n],
                          rstd3_ready, step_at)

            def finish(gi, b, n):
                pool.wait_ge(zn_ready, gi + 1)
                pool.wait_ge(out_written[b], gi * 8 - (8 * b))
                zb, ob = z[:, b, 0:n, :], o[:, b, 0:n, :]
                bc = lambda a: a[:].unsqueeze(1).to_broadcast([P, n, D])
                nc.gpsimd.tensor_tensor(ob, zb, bc(gamma), ALU.mult).then_inc(fin_step, 1)
                pool.wait_ge(fin_step, gi * 2 + 1)
                nc.gpsimd.tensor_tensor(ob, ob, bc(beta), ALU.add).then_inc(fin_step, 1)
                pool.wait_ge(fin_step, gi * 2 + 2)
                nc.gpsimd.tensor_tensor(ob, ob, x[:, bass.ds(gi * 2, n), :], ALU.add).then_inc(o_ready, 1)

            pool.wait_ge(xlt_ready, KH * NT)
            nc.gpsimd.tensor_copy(xs_hi[:, 0, :, :], acc[:, :, 0:TG]).then_inc(xshi_ready, 1)
            nc.gpsimd.tensor_copy(xs_hi[:, 1, :, :], acc[:, :, TG:2 * TG]).then_inc(xshi_ready, 1)
            for k in range(TOP_K):
                pool.wait_ge(w2hi_ready, k + 1)
                half = slice(k * NF, k * NF + NF)
                nc.gpsimd.tensor_tensor(w2_lo[:, half, :], w2_raw[:, half, :], w2_hi[:, half, :].bitcast(F32),
                                        ALU.subtract).then_inc(w2lo_ready, 1)
            pool.wait_ge(b2_ready, 1)
            pool.wait_ge(bc_in, 32)
            pool.wait_ge(xl_ready, NT)
            add_b2(0, 2)
            base_steps = steps[0]

            def step(gi, b, first=False):
                if not isinstance(gi, int) or gi + 2 < NG:
                    pool.wait_ge(ffn1_done, gi * NU + NU)
                    nc.gpsimd.tensor_copy(xs_hi[:, b, :, :], acc[:, :, bass.ds(gi * TG + 2 * TG, TG)]
                                          ).then_inc(xshi_ready, 1)
                if not isinstance(gi, int) or gi + 1 < NG:
                    add_b2(gi + 1, 1 if isinstance(gi, int) and gi + 1 == NG - 1 else 2)
                if not first:
                    finish(gi - 1, 1 - b, 2)
                rstd_out(gi, b, 1 if isinstance(gi, int) and gi == NG - 1 else 2, gi + (base_steps + 1))

            step(0, 0, first=True)
            with pool.Fori(0, 5) as i:
                step(2 * i + 1, 1)
                step(2 * i + 2, 0)
            step(11, 1)
            step(12, 0)
            finish(12, 0, 1)

        @block.scalar
        def _(act):
            act.sem_inc(even_out, 2)
            act.sem_inc(gelu_done, NU)
            def hi_part(t, b):
                act.wait_ge(tp_ready, t + 1)
                nc.scalar.activation(ht_hi[:, b, :], bank[4][:, 0:D], ACT.Copy).then_inc(hthi_ready, 1)

            def evacuate(t, b, c):
                act.wait_ge(mm_done, t * NCG + (c + 1))
                nc.scalar.activation(t_stage[:, b, c * 512:(c + 1) * 512], bank[c % 4][:], ACT.Copy
                                     ).then_inc(even_out, 1)

            act.wait_ge(w_in_sem[0], 16 * KH)
            nc.scalar.activation(w_hi[:, 0, :, :], w_raw[:, 0, :, :], ACT.Copy).then_inc(whi_ready, 1)
            hi_part(0, 0)
            for c in range(1, NCG):
                act.wait_ge(w_in_sem[c], 16 * KH)
                nc.scalar.activation(w_hi[:, c, :, :], w_raw[:, c, :, :], ACT.Copy).then_inc(whi_ready, 1)
                if c in (3, 5, 7):
                    evacuate(0, 0, c - 3)
            hi_part(1, 1)
            evacuate(0, 0, 6)

            act.wait_ge(rows_filled, 4)
            for rows, src in ((src_rows, src_in), (rel_rows, rel_in), (dst_rows, dst_in),
                              (norm_rows, norm_in.rearrange("e one -> (e one)"))):
                lo, full = NCH // 32 * 32, NCH - 1
                act.dma_start(rows[0:lo, :], flat(src[0:lo * CHUNK])).then_inc(edges_in, 16)
                act.dma_start(rows[lo:full, :], flat(src[lo * CHUNK:full * CHUNK])).then_inc(edges_in, 16)
                act.dma_start(rows[full:NCH, 0:TAIL], src[full * CHUNK:N_EDGES].unsqueeze(0)).then_inc(edges_in, 16)
            act.dma_start(b1_rows[:], b1_in.rearrange("e (j p) -> (e j) p", p=P)).then_inc(consts_in, 16)
            act.dma_start(wr[:], wr_in.rearrange("(h p) e -> p h e", p=P)).then_inc(consts_in, 16)
            act.dma_start(br[:], br_in.unsqueeze(0)).then_inc(consts_in, 16)
            act.dma_start(gamma[:], gamma_in.unsqueeze(0).to_broadcast([P, D])).then_inc(bc_in, 16)
            act.dma_start(beta[:], beta_in.unsqueeze(0).to_broadcast([P, D])).then_inc(bc_in, 16)

            def tile_a(t, b, last=False):
                act.wait_ge(t_written[b], t * 8 - 8 * b)
                evacuate(t, b, 0)
                evacuate(t, b, 2)
                if not last:
                    hi_part(t + 1, 1 - b)
                evacuate(t, b, 4)
                evacuate(t, b, 6)

            with act.Fori(0, (NT - 3) // 2) as i:
                tile_a(2 * i + 1, 1)
                tile_a(2 * i + 2, 0)
            tile_a(NT - 2, 1)
            tile_a(NT - 1, 0, last=True)

            def tile_cols(b):
                return bank[b][:, 0:CT * NCH].rearrange("p (j c) -> p c j", j=CT)

            act.wait_ge(meta_tp, 1)
            nc.scalar.activation(idx_col[:], tile_cols(5), ACT.Copy).then_inc(idx_copied, 1)
            act.wait_ge(meta_tp, 2)
            nc.scalar.activation(norm_col[:], tile_cols(7), ACT.Copy).then_inc(meta_copied, 1)

            act.wait_ge(idx_copied, 1)

            def place_indices(i, ks=range(SLOTS)):
                for k in ks:
                    act.wait_ge(gathered[k], i * 64)
                    nc.scalar.activation(idx_now[:, k, :], idx_col[:, bass.ds(i * SLOTS + k, 1), :].rearrange(
                        "p a b -> p (a b)"), ACT.Copy).then_inc(idx_now_ready, 1)

            def stage(t):
                act.wait_ge(acc_tp, t)
                nc.scalar.activation(acc_stage[:].rearrange("p (h n) -> p h n", h=KH),
                                     acc[:, :, bass.ds(t * P, P)], ACT.Copy).then_inc(staged, 1)

            def keep(t):
                act.wait_ge(xn2_ready, t + 1)
                nc.scalar.activation(xl[:, bass.ds(t, 1), :].rearrange("p a d -> p (a d)"), xn[:], ACT.Copy
                                     ).then_inc(xl_ready, 1)
                act.wait_ge(xl_tp, t + 1)
                for h in range(KH):
                    nc.scalar.activation(acc[:, h, bass.ds(t * P, P)], bank[3][:, h * P:(h + 1) * P], ACT.Copy,
                                         accum_out=mean_sum[:, h, bass.ds(t, 1)]).then_inc(xlt_ready, 1)

            act.wait_ge(meta_copied, 5)
            general = act.value_load(w0_row[0:1, NCH:NCH + 1], min_val=0, max_val=1)
            with act.If(general):
                with act.Fori(0, NIT) as i:
                    place_indices(i)
                act.wait_ge(acc_final, 1)
                with act.Fori(0, NT) as t:
                    stage(t)
                    keep(t)
            with act.Else():
                with act.Fori(0, LAG) as i:
                    place_indices(i)
                place_indices(LAG, (0, 1))
                with act.Fori(0, NIT - LAG - 1) as t:
                    place_indices(t + LAG, (2, 3))
                    act.wait_ge(acc_added, t * SLOTS + (LAG * SLOTS + 2))
                    stage(t)
                    place_indices(t + (LAG + 1), (0, 1))
                    keep(t)
                place_indices(NIT - 1, (2, 3))
                act.wait_ge(acc_added, (NIT - 1) * SLOTS + 2)
                stage(NIT - LAG - 1)
                keep(NIT - LAG - 1)
                act.wait_ge(acc_added, NCH + 2)
                for t in range(NIT - LAG, NT):
                    stage(t)
                    keep(t)
            act.wait_ge(b1_tp, 1)
            nc.scalar.activation(b1t[:], bank[4][:, 0:N_EXPERTS * NF], ACT.Copy).then_inc(b1t_ready, 1)

            act.wait_ge(route, 3)
            nc.scalar.activation(rt[:, 2, :], rt[:, 0, :], ACT.Exp, bias=rt[:, 1, 0:1], accum_out=rt[:, 3, 0:1]
                                 ).then_inc(exp_done, 1)
            act.wait_ge(route, 10)
            nc.scalar.activation(rt[:, 8, :], rt[:, 6, :], ACT.Exp, bias=rt[:, 7, 0:1], accum_out=rt[:, 9, 0:1]
                                 ).then_inc(exp_done, 1)
            act.wait_ge(route, 14)
            nc.scalar.activation(rt[:, 13, 0:TOP_K], rt[:, 11, 0:TOP_K], ACT.Exp, bias=rt[:, 12, 0:1],
                                 accum_out=rt[:, 14, 0:1]).then_inc(exp_done, 1)
            act.wait_ge(idx_ready, 1)
            for k in range(TOP_K):
                e = act.value_load(top_i[0:1, k:k + 1], min_val=0, max_val=N_EXPERTS - 1)
                nc.scalar.activation(b1s[:, k * NF:(k + 1) * NF], b1t[:, bass.ds(e * NF, NF)], ACT.Copy
                                     ).then_inc(b1s_ready, 1)
            for k in range(TOP_K):
                act.wait_ge(w1_got[k], 16)
                nc.scalar.activation(w1_hi[:, k, :, :], w1_raw[:, k, :, :], ACT.Copy).then_inc(w1hi_ready, 1)
            for k in range(TOP_K):
                act.wait_ge(w2s_ready, k + 1)
                half = slice(k * NF, k * NF + NF)
                nc.scalar.activation(w2_hi[:, half, :], w2_raw[:, half, :], ACT.Copy).then_inc(w2hi_ready, 1)
            act.wait_ge(b1s_ready, TOP_K)

            def gelu_group(gi, b):
                for u in range(NU):
                    act.wait_ge(ffn1_done, gi * NU + (u + 1))
                    act.wait_ge(glo_ready, gi * NU + (u + 1))
                    for v in range(2):
                        q = 2 * u + v
                        last = nc.scalar.activation(g[:, u % 2, v, :], bank[u][:, v * TG:(v + 1) * TG], ACT.Gelu,
                                                    bias=b1s[:, q:q + 1])
                    last.then_inc(gelu_done, 1)
                    act.wait_ge(gelu_done, gi * NU + (NU + u + 1))
                    if u == 0:
                        act.wait_ge(ffn2_done, gi * 2)
                    nc.scalar.activation(g_hi[:, b, 2 * u:2 * u + 2, :], g[:, u % 2, :, :], ACT.Copy
                                         ).then_inc(ghi_ready, 1)

            gelu_group(0, 0)
            gelu_group(1, 1)
            with act.Fori(0, 5) as i:
                gelu_group(2 * i + 2, 0)
                gelu_group(2 * i + 3, 1)
            gelu_group(12, 0)

        @block.vector
        def _(dve):
            dve.sem_inc(odd_out, 2)
            dve.sem_inc(acc_added, 2)
            dve.sem_inc(glo_ready, 2)
            dve.sem_inc(z_ready, 2)

            def stats(t, b):
                nc.vector.bn_stats(stat[:, 0, :], x[:, bass.ds(t, 1), :].rearrange("p a d -> p (a d)")
                                   ).then_inc(stat_ready, 1)
                dve.wait_ge(stat_ready, t + 1)
                nop_waits(dve)
                nc.vector.bn_aggr(mv1[:, b, :], stat[:, 0, :]).then_inc(mv_ready, 1)

            def norm(t, b):
                dve.wait_ge(rstd_ready, t + 1)
                dve.wait_ge(tp_ready, t)
                nc.vector.tensor_scalar(xn[:], x[:, bass.ds(t, 1), :].rearrange("p a d -> p (a d)"),
                                        mv1[:, b, 0:1], rstd1[:, bass.ds(t, 1)],
                                        ALU.subtract, ALU.mult).then_inc(xn_ready, 1)

            def lo_part(t, b):
                dve.wait_ge(hthi_ready, t + 1)
                nc.vector.tensor_tensor(ht_lo[:, b, :], bank[4][:, 0:D], ht_hi[:, b, :].bitcast(F32), ALU.subtract
                                        ).then_inc(htlo_ready, 1)

            def evacuate(t, b, c):
                dve.wait_ge(mm_done, t * NCG + (c + 1))
                nc.vector.tensor_copy(t_stage[:, b, c * 512:(c + 1) * 512], bank[c % 4][:]).then_inc(odd_out, 1)

            dve.wait_ge(x0_in, 16)
            stats(0, 0)
            norm(0, 0)

            def w_low(c):
                dve.wait_ge(w_in_sem[c], 16 * KH)
                dve.wait_ge(whi_ready, c + 1)
                nc.vector.tensor_tensor(w_lo[:, c, :, :], w_raw[:, c, :, :], w_hi[:, c, :, :].bitcast(F32),
                                        ALU.subtract).then_inc(wlo_even, 1)

            w_low(0)
            lo_part(0, 0)
            w_low(2)
            w_low(4)
            evacuate(0, 0, 1)
            w_low(6)
            dve.wait_ge(x12_in, 16)
            stats(1, 1)
            evacuate(0, 0, 3)
            norm(1, 1)
            evacuate(0, 0, 5)
            lo_part(1, 1)
            evacuate(0, 0, 7)
            dve.wait_ge(x_in_sem, 48)

            def tile_a(t, b, last=False):
                if not last:
                    stats(t + 1, 1 - b)
                dve.wait_ge(t_written[b], t * 8 - 8 * b)
                evacuate(t, b, 1)
                if not last:
                    norm(t + 1, 1 - b)
                evacuate(t, b, 3)
                evacuate(t, b, 5)
                if not last:
                    lo_part(t + 1, 1 - b)
                evacuate(t, b, 7)

            with dve.Fori(0, (NT - 3) // 2) as i:
                tile_a(2 * i + 1, 1)
                tile_a(2 * i + 2, 0)
            tile_a(NT - 2, 1)

            meta = [0]

            def after(ins):
                meta[0] += 1
                ins.then_inc(dve_meta, 1)
                dve.wait_ge(dve_meta, meta[0])

            dve.wait_ge(edge_math, 1)
            after(nc.vector.tensor_reduce(w0_rows[:, 0:1], dstf_rows[:], AX.X, ALU.min))
            after(nc.vector.tensor_scalar(pos_rows[:], dstf_rows[:], w0_rows[:, 0:1], None, ALU.subtract))
            after(nc.vector.tensor_scalar(srcf_rows[:], dstf_rows[:], float(NO_NODE // 2), None, ALU.is_lt))
            after(nc.vector.scalar_tensor_tensor(out=miss_rows[:], in0=pos_rows[:], scalar=float(WIN),
                                                 in1=srcf_rows[:], op0=ALU.is_ge, op1=ALU.mult))
            after(nc.vector.tensor_reduce(w0_rows[:, 1:2], miss_rows[:], AX.X, ALU.max))
            dve.wait_ge(consts_ready, 1)
            after(nc.vector.tensor_scalar(thr_i[:, 1:2], thr_i[:, 0:1], SLOTS.bit_length() - 1, None,
                                          ALU.arith_shift_right))
            after(nc.vector.tensor_scalar(thr[:, 0:1], thr_i[:, 1:2], float(P), float(P * (1 - LAG)), ALU.mult,
                                          ALU.add))
            after(nc.vector.tensor_tensor(thr[:, 1:2], w0_rows[:, 0:1], thr[:, 0:1], ALU.is_lt))
            after(nc.vector.tensor_tensor(w0_rows[:, 1:2], w0_rows[:, 1:2], thr[:, 1:2], ALU.max))
            tile_a(NT - 1, 0, last=True)

            def tile_cols(b):
                return bank[b][:, 0:CT * NCH].rearrange("p (j c) -> p c j", j=CT)

            dve.wait_ge(meta_tp, 3)
            nc.vector.tensor_copy(rel_pos[:], tile_cols(6)).then_inc(meta_copied, 1)
            dve.wait_ge(meta_tp, 4)
            nc.vector.tensor_copy(dst_col[:], tile_cols(5)).then_inc(meta_copied, 1)
            dve.wait_ge(meta_tp, 5)
            nc.vector.tensor_copy(w0_row[:, 0:NCH], bank[4][0:1, 256:256 + NCH]).then_inc(meta_copied, 1)
            nc.vector.tensor_scalar(w0_row[:, NCH:NCH + 1], bank[4][0:1, 256 + NCH:257 + NCH], 0.5, None, ALU.is_gt
                                    ).then_inc(meta_copied, 1)

            dve.wait_ge(meta_copied, 5)
            dve.wait_ge(consts_ready, 2)
            dve.wait_ge(acc_zeroed, 1)

            def weigh(i, ks=range(SLOTS)):
                for k in ks:
                    c = bass.ds(i * SLOTS + k, 1)
                    for j in range(CT):
                        last = nc.vector.tensor_scalar(sel[:, k, j, :], iota[:], rel_pos[:, c, j], norm_col[:, c, j],
                                                       ALU.is_equal, ALU.mult)
                    last.then_inc(sel_ready, 1)

            def add_chunk(i, k):
                w0 = dve.value_load(w0_row[0:1, bass.ds(i * SLOTS + k, 1)], min_val=0, max_val=N_NODES - 1)
                dve.wait_ge(chunk_summed, i * SLOTS + (SLOTS + k + 1))
                dve.wait_ge(acc_added, i * SLOTS + (k + 2))
                window = acc[:, :, bass.ds(w0, WIN)]
                nc.vector.tensor_tensor(window, window, bank[6 + k % 2][:, 0:KH * WIN].rearrange(
                    "p (h w) -> p h w", h=KH), ALU.add).then_inc(acc_added, 1)

            def chunks(i):
                weigh(i)
                for k in range(SLOTS):
                    add_chunk(i, k)

            def add_messages(t):
                dve.wait_ge(acc_tp, t + 1)
                tile = x[:, bass.ds(t, 1), :].rearrange("p a d -> p (a d)")
                nc.vector.tensor_tensor(tile, tile, bank[5][:, 0:D], ALU.add).then_inc(x1_ready, 1)
                dve.wait_ge(x1_ready, t + 1)
                nop_waits(dve)
                nc.vector.bn_stats(stat[:, 0, :], tile).then_inc(stat2_ready, 1)
                dve.wait_ge(stat2_ready, t * 2 + 1)
                nop_waits(dve)
                nc.vector.bn_aggr(mv2[:], stat[:, 0, :]).then_inc(stat2_ready, 1)

            def normalise(t):
                dve.wait_ge(stat2_ready, t * 2 + 2)
                n = [0]

                def then(ins):
                    n[0] += 1
                    ins.then_inc(newton, 1)
                    dve.wait_ge(newton, t * NEWTON + n[0])

                ve, y, m = root[:, 0:1], root[:, 1:2], root[:, 2:3]
                then(nc.vector.tensor_scalar(ve, mv2[:, 1:2], LN_EPS, None, ALU.add))
                then(nc.vector.tensor_scalar(y.bitcast(I32), ve.bitcast(I32), -0.5, 1597463007.0, ALU.mult, ALU.add))
                for _ in range(3):
                    then(nc.vector.tensor_tensor(m, y, y, ALU.mult))
                    then(nc.vector.scalar_tensor_tensor(out=m, in0=m, scalar=-0.5, in1=ve, op0=ALU.mult, op1=ALU.mult))
                    then(nc.vector.scalar_tensor_tensor(out=y, in0=m, scalar=1.5, in1=y, op0=ALU.add, op1=ALU.mult))
                assert n[0] == NEWTON
                dve.wait_ge(xl_tp, t)
                dve.wait_ge(xl_ready, t)
                nc.vector.tensor_scalar(xn[:], x[:, bass.ds(t, 1), :].rearrange("p a d -> p (a d)"),
                                        mv2[:, 0:1], y, ALU.subtract, ALU.mult).then_inc(xn2_ready, 1)

            general = dve.value_load(w0_row[0:1, NCH:NCH + 1], min_val=0, max_val=1)
            with dve.If(general):
                with dve.Fori(0, NIT) as i:
                    chunks(i)
                dve.wait_ge(acc_added, NCH + 2)
                dve.wait_ge(t_written[0], 16 * (NT // 2 + NCG // 2))
                dve.wait_ge(t_written[1], 16 * (NT // 2))
                line = fb_iota[:].rearrange("p a b -> p (a b)")
                nc.vector.tensor_copy(line[:, 0:WIN], iota[:]).then_inc(fb_added, 1)
                done, filled = 1, WIN
                dve.wait_ge(fb_added, done)
                while filled < NFB * FBW:
                    n = min(filled, NFB * FBW - filled)
                    nc.vector.tensor_scalar(line[:, filled:filled + n], line[:, 0:n], float(filled), None, ALU.add
                                            ).then_inc(fb_added, 1)
                    done += 1
                    dve.wait_ge(fb_added, done)
                    filled += n
                nc.vector.scalar_tensor_tensor(out=fb_norm[:], in0=rel_pos[:], scalar=float(WIN), in1=norm_col[:],
                                               op0=ALU.is_ge, op1=ALU.mult).then_inc(fb_added, 1)
                done += 1
                dve.wait_ge(fb_added, done)
                with dve.Fori(0, NCH) as c:
                    with dve.Fori(0, NFB) as w:
                        s = c * NFB + w
                        for j in range(CT):
                            last = nc.vector.tensor_scalar(
                                fb_sel[:, j, :], fb_iota[:, bass.ds(w, 1), :].rearrange("p a b -> p (a b)"),
                                dst_col[:, bass.ds(c, 1), j], fb_norm[:, bass.ds(c, 1), j], ALU.is_equal, ALU.mult)
                        last.then_inc(fb_sel_ready, 1)
                        dve.wait_ge(fb_summed, s + 1)
                        for h in range(KH):
                            cols = acc[:, h, bass.ds(w * FBW, FBW)]
                            nc.vector.tensor_tensor(cols, cols, bank[6 + h][:, 0:FBW], ALU.add
                                                    ).then_inc(fb_added, 1)
                        dve.wait_ge(fb_added, s * KH + (done + KH))
                dve.drain().then_inc(acc_final, 1)
                with dve.Fori(0, NT) as t:
                    add_messages(t)
                    normalise(t)
            with dve.Else():
                with dve.Fori(0, LAG) as i:
                    chunks(i)
                with dve.Fori(0, NIT - LAG) as t:
                    weigh(t + LAG, (0, 1))
                    add_messages(t)
                    weigh(t + LAG, (2,))
                    normalise(t)
                    add_chunk(t + LAG, 0)
                    weigh(t + LAG, (3,))
                    for k in range(1, SLOTS):
                        add_chunk(t + LAG, k)
                for t in range(NIT - LAG, NT):
                    add_messages(t)
                    normalise(t)

            n_route = [0]

            def routed(ins):
                n_route[0] += 1
                ins.then_inc(route, 1)
                dve.wait_ge(route, n_route[0])

            V = nc.vector
            dve.wait_ge(xlt_ready, KH * NT)
            V.tensor_reduce(mean[:], mean_sum[:], AX.X, ALU.add).then_inc(mean_ready, 1)
            dve.wait_ge(mean_ready, 1)
            V.tensor_scalar(mean[:], mean[:], 1.0 / N_NODES, None, ALU.mult).then_inc(mean_ready, 1)
            dve.wait_ge(logits_ready, 1)
            dve.wait_ge(consts_in, 48)
            routed(V.tensor_tensor(rt[:, 0, :], bank[5][0:1, 0:N_EXPERTS], br[:], ALU.add))
            routed(V.tensor_reduce(rt[:, 1, 1:2], rt[:, 0, :], AX.X, ALU.max))
            routed(V.tensor_scalar(rt[:, 1, 0:1], rt[:, 1, 1:2], -1.0, None, ALU.mult))
            dve.wait_ge(exp_done, 1)
            routed(V.reciprocal(rt[:, 3, 1:2], rt[:, 3, 0:1]))
            routed(V.tensor_scalar(rt[:, 4, :], rt[:, 2, :], rt[:, 3, 1:2], None, ALU.mult))
            routed(V.tensor_scalar(rt[:, 5, :], rt[:, 4, :], float(N_NODES), None, ALU.mult))
            routed(V.reciprocal(rt[:, 15, :], rt[:, 5, :]))
            routed(V.tensor_scalar(rt[:, 5, :], rt[:, 15, :], CAPACITY, 1.0, ALU.mult, ALU.min))
            routed(V.tensor_tensor(rt[:, 6, :], rt[:, 4, :], rt[:, 5, :], ALU.mult))
            V.tensor_reduce(rt[:, 7, 1:2], rt[:, 6, :], AX.X, ALU.max).then_inc(mean_ready, 1)
            dve.wait_ge(mean_ready, 3)
            routed(V.tensor_scalar(rt[:, 7, 0:1], rt[:, 7, 1:2], -1.0, None, ALU.mult))
            dve.wait_ge(exp_done, 2)
            routed(V.reciprocal(rt[:, 9, 1:2], rt[:, 9, 0:1]))
            routed(V.tensor_scalar(rt[:, 10, :], rt[:, 8, :], rt[:, 9, 1:2], None, ALU.mult))
            routed(V.max(rt[:, 11, :], rt[:, 10, :]))
            V.max_index(top_i[:], rt[:, 11, :], rt[:, 10, :]).then_inc(idx_ready, 1)
            routed(V.tensor_scalar(rt[:, 12, 0:1], rt[:, 11, 0:1], -1.0, None, ALU.mult))
            dve.wait_ge(exp_done, 3)
            routed(V.reciprocal(rt[:, 14, 1:2], rt[:, 14, 0:1]))
            dve.wait_ge(consts_ready, 1)
            for k in range(TOP_K):
                routed(V.tensor_scalar(rt[:, 15, k:k + 1], rt[:, 13, k:k + 1], rt[:, 14, 1:2], None, ALU.mult))
            for k in range(TOP_K):
                V.tensor_scalar(w_rows[:, k, :], ones[0:1, :], rt[:, 15, k:k + 1], None, ALU.mult).then_inc(wts_ready, 1)

            def w1_lo_part(k):
                dve.wait_ge(w1hi_ready, k + 1)
                V.tensor_tensor(w1_lo[:, k, :, :], w1_raw[:, k, :, :], w1_hi[:, k, :, :].bitcast(F32), ALU.subtract
                                ).then_inc(w1lo_ready, 1)

            def token_lo(gi, b):
                dve.wait_ge(xshi_ready, gi + 1)
                V.tensor_tensor(xs_lo[:, b, :, :], acc[:, :, bass.ds(gi * TG, TG)], xs_hi[:, b, :, :].bitcast(F32),
                                ALU.subtract).then_inc(xslo_ready, 1)

            token_lo(0, 0)
            token_lo(1, 1)
            w1_lo_part(0)
            dve.wait_ge(wcol_ps, 1)
            V.tensor_copy(w_cols[:], bank[5][:, 16:16 + TOP_K]).then_inc(wcol_ready, 1)
            dve.wait_ge(wcol_ready, 1)
            for k in range(TOP_K):
                dve.wait_ge(w2_got[k], 16)
                half = w2_raw[:, k * NF:(k + 1) * NF, :]
                V.tensor_scalar(half, half, w_cols[:, k:k + 1], None, ALU.mult).then_inc(w2s_ready, 1)
                if k == 0:
                    w1_lo_part(1)
            dve.wait_ge(b2_ps, 1)
            V.tensor_copy(b2c[:], bank[6][:, 0:D]).then_inc(b2_ready, 1)

            def gelu_lo(gi, b, u):
                dve.wait_ge(ghi_ready, gi * NU + (u + 1))
                V.tensor_tensor(g_lo[:, b, 2 * u:2 * u + 2, :], g[:, u % 2, :, :],
                                g_hi[:, b, 2 * u:2 * u + 2, :].bitcast(F32), ALU.subtract).then_inc(glo_ready, 1)

            def residual(gi, b, n):
                if not isinstance(gi, int) or gi >= 2:
                    dve.wait_ge(o_ready, gi - 1)
                dve.wait_ge(xlb_ready, gi + 1)
                for s in range(n):
                    dve.wait_ge(ffn2_done, gi * 2 + (s + 1 + 2))
                    V.tensor_tensor(z[:, b, s, :], bank[4 + s][:, 0:D],
                                    xl[:, bass.ds(gi * 2 + s, 1), :].rearrange("p a d -> p (a d)"), ALU.add
                                    ).then_inc(z_ready, 1)
                for s in range(n):
                    dve.wait_ge(z_ready, gi * 2 + (s + 1 + 2))
                    V.bn_stats(stat[:, s, :], z[:, b, s, :]).then_inc(stat3_ready, 1)
                dve.wait_ge(stat3_ready, gi * 2 + n)
                nop_waits(dve)
                for s in range(n):
                    last = V.bn_aggr(mv3[:, b, s, :], stat[:, s, :])
                last.then_inc(mv3_ready, 1)

            def norm_out(gi, b, n):
                dve.wait_ge(rstd3_ready, gi + 1)
                for s in range(n):
                    last = V.tensor_scalar(z[:, b, s, :], z[:, b, s, :], mv3[:, b, s, 0:1],
                                           rstd3[:, bass.ds(gi * 2 + s, 1)], ALU.subtract, ALU.mult)
                last.then_inc(zn_ready, 1)

            for u in range(NU):
                gelu_lo(0, 0, u)

            def step(gi, b, first=False):
                if not isinstance(gi, int) or gi + 1 < NG:
                    gelu_lo(gi + 1, 1 - b, 0)
                    gelu_lo(gi + 1, 1 - b, 1)
                if not first:
                    norm_out(gi - 1, 1 - b, 2)
                if not isinstance(gi, int) or gi + 1 < NG:
                    gelu_lo(gi + 1, 1 - b, 2)
                    gelu_lo(gi + 1, 1 - b, 3)
                if not isinstance(gi, int) or gi + 2 < NG:
                    token_lo(gi + 2, b)
                residual(gi, b, 1 if isinstance(gi, int) and gi == NG - 1 else 2)

            step(0, 0, first=True)
            with dve.Fori(0, 5) as i:
                step(2 * i + 1, 1)
                step(2 * i + 2, 0)
            step(11, 1)
            step(12, 0)
            norm_out(12, 0, 1)

        @block.tensor
        def _(pe):
            pe.sem_inc(chunk_summed, SLOTS)
            pe.sem_inc(ffn2_done, 2)
            mm = nc.tensor.matmul

            def split_product(out_ap, a_hi, a_lo, b_hi, b_lo, first, last):
                mm(out_ap, a_lo, b_hi, start=first, stop=False)
                mm(out_ap, a_hi, b_lo, start=False, stop=False)
                return mm(out_ap, a_hi, b_hi, start=False, stop=last)

            def transposes(t, ready, src, bank_ap, done):
                pe.wait_ge(ready, t + 1)
                for h in range(KH):
                    last = nc.tensor.transpose(bank_ap[:, h * P:(h + 1) * P], src[:, h * P:(h + 1) * P], ident[:])
                last.then_inc(done, 1)

            def tile_a(t, b, last=False):
                pe.wait_ge(htlo_ready, t + 1)
                for c in range(NCG):
                    if c == NCG // 2 and not last:
                        transposes(t + 1, xn_ready, xn, bank[4], tp_ready)
                    pe.wait_ge(wlo_even if c % 2 == 0 else wlo_odd, c // 2 + 1)
                    pe.wait_ge(even_out if c % 2 == 0 else odd_out, t * (NCG // 2) + (c // 2 + 1))
                    for kh in range(KH):
                        rows = slice(kh * P, (kh + 1) * P)
                        done = split_product(bank[c % 4][:], ht_hi[:, b, rows], ht_lo[:, b, rows],
                                             w_hi[:, c, kh, :], w_lo[:, c, kh, :], kh == 0, kh == KH - 1)
                    done.then_inc(mm_done, 1)

            pe.wait_ge(ident_ready, 1)
            transposes(0, xn_ready, xn, bank[4], tp_ready)
            with pe.Fori(0, NT // 2) as i:
                for b in range(2):
                    tile_a(2 * i + b, b)
            tile_a(NT - 1, 0, last=True)

            def to_columns(rows, b, done):
                for j in range(CT):
                    last = nc.tensor.transpose(bank[b][:, j * NCH:(j + 1) * NCH], rows[:, j * P:(j + 1) * P],
                                               ident[0:NCH, 0:NCH])
                last.then_inc(done, 1)

            pe.wait_ge(edge_math, 1)
            to_columns(idxf_rows, 5, meta_tp)
            to_columns(norm_rows, 7, meta_tp)
            pe.wait_ge(dve_meta, 9)
            to_columns(pos_rows, 6, meta_tp)
            pe.wait_ge(idx_copied, 1)
            to_columns(dstf_rows, 5, meta_tp)
            pe.wait_ge(consts_ready, 1)
            mm(bank[4][0:1, 256:256 + NCH], w0_rows[:, 0:1], ident[0:NCH, 0:NCH], start=True, stop=True)
            mm(bank[4][0:1, 256 + NCH:257 + NCH], w0_rows[:, 1:2], ones[0:NCH, 0:1], start=True, stop=True
               ).then_inc(meta_tp, 1)

            pe.wait_ge(meta_copied, 5)
            pe.wait_ge(consts_in, 48)
            nc.tensor.transpose(bank[4][:, 0:N_EXPERTS * NF], b1_rows[:],
                                ident[0:N_EXPERTS * NF, 0:N_EXPERTS * NF]).then_inc(b1_tp, 1)

            def sum_chunks(i, ks):
                for k in ks:
                    pe.wait_ge(sel_ready, i * SLOTS + (k + 1))
                    pe.wait_ge(acc_added, i * SLOTS + (k + 1))
                    pe.wait_ge(gathered[k], i * 64 + 64)
                    for h in range(KH):
                        for j in range(CT):
                            last = mm(bank[6 + k % 2][:, h * WIN:(h + 1) * WIN], gath[:, k, j, h * P:(h + 1) * P],
                                      sel[:, k, j, :], start=j == 0, stop=j == CT - 1)
                    last.then_inc(chunk_summed, 1)

            def acc_tile(t):
                pe.wait_ge(x1_ready, t)
                transposes(t, staged, acc_stage, bank[5], acc_tp)

            def xl_tile(t):
                pe.wait_ge(xlt_ready, t * KH)
                transposes(t, xn2_ready, xn, bank[3], xl_tp)

            general = pe.value_load(w0_row[0:1, NCH:NCH + 1], min_val=0, max_val=1)
            with pe.If(general):
                with pe.Fori(0, NIT) as i:
                    sum_chunks(i, range(SLOTS))
                pe.wait_ge(acc_added, NCH + 2)
                with pe.Fori(0, NCH) as c:
                    with pe.Fori(0, NFB) as w:
                        pe.wait_ge(fb_gathered, c * 64 + 64)
                        pe.wait_ge(fb_sel_ready, c * NFB + w + 1)
                        for h in range(KH):
                            for j in range(CT):
                                last = mm(bank[6 + h][:, 0:FBW], gath[:, 0, j, h * P:(h + 1) * P], fb_sel[:, j, :],
                                          start=j == 0, stop=j == CT - 1)
                        last.then_inc(fb_summed, 1)
                with pe.Fori(0, NT) as t:
                    acc_tile(t)
                    xl_tile(t)
            with pe.Else():
                with pe.Fori(0, LAG) as i:
                    sum_chunks(i, range(SLOTS))
                with pe.Fori(0, NIT - LAG) as t:
                    acc_tile(t)
                    sum_chunks(t + LAG, (0, 1))
                    xl_tile(t)
                    sum_chunks(t + LAG, (2, 3))
                for t in range(NIT - LAG, NT):
                    acc_tile(t)
                    xl_tile(t)

            pe.wait_ge(mean_ready, 2)
            pe.wait_ge(b1t_ready, 1)
            for h in range(KH):
                last = mm(bank[5][0:1, 0:N_EXPERTS], mean[:, h:h + 1], wr[:, h, :], start=h == 0, stop=h == KH - 1)
            last.then_inc(logits_ready, 1)
            pe.wait_ge(wts_ready, TOP_K)
            mm(bank[5][:, 16:16 + TOP_K], ones[0:1, :], rt[:, 15, 0:TOP_K], start=True, stop=True).then_inc(wcol_ps, 1)
            pe.wait_ge(b2_got, 16 * TOP_K)
            for k in range(TOP_K):
                last = mm(bank[6][:, 0:D], w_rows[:, k, :], b2_pair[:, k, :], start=k == 0, stop=k == TOP_K - 1)
            last.then_inc(b2_ps, 1)

            def ffn1(gi, b):
                pe.wait_ge(xslo_ready, gi + 1)
                for u in range(NU):
                    if isinstance(gi, int) and gi == 0:
                        pe.wait_ge(w1lo_ready, u // (NU // TOP_K) + 1)
                    pe.wait_ge(gelu_done, gi * NU + (u + 1))
                    for v in range(2):
                        k, f = divmod(2 * u + v, NF)
                        for kh in range(KH):
                            cols = slice(f * P, (f + 1) * P)
                            last = split_product(bank[u][:, v * TG:(v + 1) * TG], w1_hi[:, k, kh, cols],
                                                 w1_lo[:, k, kh, cols], xs_hi[:, b, kh, :], xs_lo[:, b, kh, :],
                                                 kh == 0, kh == KH - 1)
                    last.then_inc(ffn1_done, 1)

            def ffn2(gi, b, n):
                pe.wait_ge(glo_ready, gi * NU + (NU + 2))
                for s in range(n):
                    pe.wait_ge(z_ready, gi * 2 + (s + 1))
                    for q in range(NQ):
                        rows = slice(s * P, (s + 1) * P)
                        last = split_product(bank[4 + s][:, 0:D], g_hi[:, b, q, rows], g_lo[:, b, q, rows],
                                             w2_hi[:, q, :], w2_lo[:, q, :], q == 0, q == NQ - 1)
                    last.then_inc(ffn2_done, 1)

            ffn1(0, 0)
            ffn1(1, 1)
            pe.wait_ge(w2lo_ready, TOP_K)
            pe.wait_ge(b2_ready, 1)
            ffn2(0, 0, 2)
            with pe.Fori(0, 5) as i:
                ffn1(2 * i + 2, 0)
                ffn2(2 * i + 1, 1, 2)
                ffn1(2 * i + 3, 1)
                ffn2(2 * i + 2, 0, 2)
            ffn1(12, 0)
            ffn2(11, 1, 2)
            ffn2(12, 0, 1)


_INS = ['x', 'src', 'dst', 'edge_type_16', 'edge_weight1', 'L0_gnn_weight', 'L0_ffn_Wr', 'L0_ffn_br', 'L0_ffn_W1',
        'L0_ffn_b1', 'L0_ffn_W2', 'L0_ffn_b2', 'L0_ffn_gamma', 'L0_ffn_beta']


def build(nc, shapes):
    args = [nc.dram_tensor(f"in_{n}_dram", s, d, kind="ExternalInput").ap() for n, (s, d) in shapes.items()]
    args.append(nc.dram_tensor("out_0_dram", (N_NODES, D), F32, kind="ExternalOutput").ap())
    gnn_ffn(nc, *args)


def kernel(**inputs):
    import concourse.bacc as _bacc
    from concourse.bass_utils import run_bass_kernel_spmd as _run

    nc = _bacc.Bacc("TRN2", target_bir_lowering=False, num_devices=1)
    arrays = {f"in_{n}_dram": np.ascontiguousarray(inputs[n]) for n in _INS}
    build(nc, {n: (arrays[f"in_{n}_dram"].shape, mybir.dt.from_np(arrays[f"in_{n}_dram"].dtype)) for n in _INS})
    r = _run(nc, [arrays], core_ids=[0])
    return r.results[0]["out_0_dram"]
```

```python
import numpy as np
import concourse.bass as bass
from concourse import mybir
from contextlib import ExitStack

F32 = mybir.dt.float32
F32R = mybir.dt.float32r
I32 = mybir.dt.int32
U32 = mybir.dt.uint32
ALU = mybir.AluOpType
ACT = mybir.ActivationFunctionType
AX = mybir.AxisListType

P = 128
N_NODES, D = 3125, 256
N_RELS = 16
N_EDGES = 53125
N_EXPERTS, D_FF, TOP_K = 8, 512, 2
LN_EPS = 1e-5
CAPACITY = float(-(-N_NODES * 5 // (4 * N_EXPERTS)))

KH = D // P
NT = -(-N_NODES // P)
LAST = N_NODES - (NT - 1) * P
TROW = N_RELS * D
NCG = TROW // 512

CHUNK = 512
NCH = -(-N_EDGES // CHUNK)
CT = CHUNK // P
TAIL = N_EDGES - (NCH - 1) * CHUNK
SLOTS = 4
WIN = 64
NO_NODE = 1 << 20
FBW = 400
NFB = -(-NT * P // FBW)
NIT = NCH // SLOTS
LAG = 3

TG = 2 * P
NG = -(-NT * P // TG)
NF = D_FF // P
NQ = TOP_K * NF
NU = NQ // 2
ACOLS = NG * TG
NEWTON = 11
assert NT % 2 == 1 and NCH % SLOTS == 0 and NG == 13


def gnn_ffn(nc, x_in, src_in, dst_in, rel_in, norm_in, w_in, wr_in, br_in, w1_in, b1_in, w2_in, b2_in,
            gamma_in, beta_in, out):
    table = nc.dram_tensor("table", [NT * P * N_RELS, D], F32, kind="Internal").ap()
    table_tiles = table.rearrange("(t p r) d -> t p (r d)", p=P, r=N_RELS)

    ctx = ExitStack()
    with ctx:
        base = [16512]

        def region(nbytes):
            at = base[0]
            base[0] = at + -(-nbytes // 32) * 32
            assert base[0] <= nc.sbuf_usable_end, base[0]
            return at

        def at(name, shape, dtype, offset):
            return nc.alloc_sbuf_tensor_at(name, shape, dtype, offset=offset)

        def sb(name, shape, dtype=F32):
            return at(name, shape, dtype, region(4 * int(np.prod(shape[1:]))))

        def sem(name):
            return ctx.enter_context(nc.semaphore(name))

        x = sb("x", [P, NT, D])
        acc = sb("acc", [P, KH, ACOLS])
        ident = sb("ident", [P, P])
        minus_half = sb("minus_half", [P, 2])
        eps = sb("eps", [P, 2])
        gamma = sb("gamma", [P, D])
        beta = sb("beta", [P, D])
        wr = sb("wr", [P, KH, N_EXPERTS])
        b1t = sb("b1t", [P, N_EXPERTS * NF])
        b1s = sb("b1s", [P, NQ])
        stat = sb("stat", [P, 2, 6])
        mv1 = sb("mv1", [P, 2, 2])
        var_eps = sb("var_eps", [P, 2])
        rstd1 = sb("rstd1", [P, NT])
        mv2 = sb("mv2", [P, 2])
        root = sb("root", [P, 3])
        thr_i = sb("thr_i", [NCH, 2], I32)
        thr = sb("thr", [NCH, 2])
        mv3 = sb("mv3", [P, 2, 2, 2])
        rstd3 = sb("rstd3", [P, 2 * NG])
        pair_root = sb("pair_root", [P, 2, 2])
        iota_i = sb("iota_i", [P, WIN], I32)
        iota = sb("iota", [P, WIN])
        idx_col = sb("idx_col", [P, NCH, CT], I32)
        norm_col = sb("norm_col", [P, NCH, CT])
        idx_now = sb("idx_now", [P, SLOTS, CT], I32)
        w0_row = sb("w0_row", [1, NCH + 1], I32)
        xn = sb("xn", [P, D])
        ht_hi = sb("ht_hi", [P, 2, D], F32R)
        ht_lo = sb("ht_lo", [P, 2, D], F32R)
        acc_stage = sb("acc_stage", [P, D])
        xs_hi = sb("xs_hi", [P, 2, KH, TG], F32R)
        xs_lo = sb("xs_lo", [P, 2, KH, TG], F32R)
        r_g = region(4 * 4 * TG)
        g = at("g", [P, 2, 2, TG], F32, r_g)
        pair_stage = at("pair_stage", [P, 2, D], F32, r_g)
        pair_xn = at("pair_xn", [P, 2, D], F32, r_g + 8 * D)

        r_big = region(65536)
        w_hi = at("w_hi", [P, NCG, KH, 512], F32R, r_big)
        w_lo = at("w_lo", [P, NCG, KH, 512], F32R, r_big + 32768)
        w1_hi = at("w1_hi", [P, TOP_K, KH, D_FF], F32R, r_big)
        w1_lo = at("w1_lo", [P, TOP_K, KH, D_FF], F32R, r_big + 8192)
        w2_hi = at("w2_hi", [P, NQ, D], F32R, r_big + 16384)
        w2_lo = at("w2_lo", [P, NQ, D], F32R, r_big + 24576)
        w1_all = at("w1_all", [P, N_EXPERTS, KH, D_FF], F32, r_big + 32768)
        g_hi = at("g_hi", [P, 2, NQ, TG], F32R, r_big + 32768)
        g_lo = at("g_lo", [P, 2, NQ, TG], F32R, r_big + 49152)
        r_cols = region(4096)
        rel_pos = at("rel_pos", [P, NCH, CT], F32, r_cols)
        dst_col = at("dst_col", [P, NCH, CT], F32, r_cols + 1664)
        z = at("z", [P, 2, 2, D], F32, r_cols)
        r_sel = region(4096)
        sel = at("sel", [P, SLOTS, CT, WIN], F32, r_sel)
        o = at("o", [P, 2, 2, D], F32, r_sel)
        r_stage = region(32768)
        w_raw = at("w_raw", [P, NCG, KH, 512], F32, r_stage)
        t_stage = at("t_stage", [P, 2, TROW], F32, r_stage)
        xl = at("xl", [P, 2 * NG, D], F32, r_stage)
        fb_iota = at("fb_iota", [P, NFB, FBW], F32, r_stage + 1600)
        fb_sel = at("fb_sel", [P, CT, FBW], F32, r_stage + 1600 + 12800)
        fb_norm = at("fb_norm", [P, NCH, CT], F32, r_stage + 1600 + 12800 + 6400)
        r_gather = region(16384)
        gath = at("gath", [P, SLOTS, CT, D], F32, r_gather)
        src_rows = at("src_rows", [NCH, CHUNK], I32, r_gather)
        rel_rows = at("rel_rows", [NCH, CHUNK], I32, r_gather + 2048)
        dst_rows = at("dst_rows", [NCH, CHUNK], I32, r_gather + 4096)
        norm_rows = at("norm_rows", [NCH, CHUNK], F32, r_gather + 6144)
        srcf_rows = at("srcf_rows", [NCH, CHUNK], F32, r_gather + 8192)
        idxf_rows = at("idxf_rows", [NCH, CHUNK], F32, r_gather + 10240)
        dstf_rows = at("dstf_rows", [NCH, CHUNK], F32, r_gather + 12288)
        relf_rows = at("relf_rows", [NCH, CHUNK], F32, r_gather + 14336)
        w2_raw = at("w2_raw", [P, NQ, D], F32, r_gather)
        b1_rows = sb("b1_rows", [N_EXPERTS * NF, P])
        w0_rows = sb("w0_rows", [NCH, 2])
        ones = sb("ones", [P, P])
        mean_sum = sb("mean_sum", [P, KH, NT])
        mean = sb("mean", [P, KH])
        rt = sb("rt", [1, 16, N_EXPERTS])
        warm = sb("warm", [1, 2])
        top_i = sb("top_i", [1, 8], U32)
        b2_pair = sb("b2_pair", [1, TOP_K, D])
        w_rows = sb("w_rows", [1, TOP_K, P])
        w_cols = sb("w_cols", [P, TOP_K])
        b2c = sb("b2c", [P, D])
        br = sb("br", [1, N_EXPERTS])

        pos_rows = at("pos_rows", [NCH, CHUNK], F32, r_gather + 2048)
        miss_rows = at("miss_rows", [NCH, CHUNK], F32, r_gather)

        bank = [ctx.enter_context(nc.psum_tensor(f"bank{i}", [P, 512], F32)) for i in range(8)]

        x01_in, x23_in, x_in_sem, edges_in, consts_in = sem("x01_in"), sem("x23_in"), sem("x_in"), sem("edges_in"), sem("consts_in")
        bc_in = sem("bc_in")
        w_in_sem = [sem(f"w_in{c}") for c in range(NCG)]
        x_zeroed, rows_filled, ident_ready = sem("x_zeroed"), sem("rows_filled"), sem("ident_ready")
        pool_step = sem("pool_step")
        consts_ready = sem("consts_ready")
        whi_ready, wlo_even, wlo_odd = sem("whi_ready"), sem("wlo_even"), sem("wlo_odd")
        stat_ready, mv_ready, rstd_ready, xn_ready = sem("stat_ready"), sem("mv_ready"), sem("rstd_ready"), sem("xn_ready")
        tp_ready, hthi_ready, htlo_ready = sem("tp_ready"), sem("hthi_ready"), sem("htlo_ready")
        mm_done, even_out, odd_out = sem("mm_done"), sem("even_out"), sem("odd_out")
        t_written = [sem("t_written0"), sem("t_written1")]
        edge_math, dve_meta, meta_tp, meta_copied = sem("edge_math"), sem("dve_meta"), sem("meta_tp"), sem("meta_copied")
        idx_copied, acc_zeroed = sem("idx_copied"), sem("acc_zeroed")
        idx_now_ready = sem("idx_now_ready")
        gathered = [sem(f"gathered{k}") for k in range(SLOTS)]
        sel_ready, chunk_summed, acc_added = sem("sel_ready"), sem("chunk_summed"), sem("acc_added")
        fb_step, fb_sel_ready, fb_summed, fb_added, fb_gathered = (
            sem("fb_step"), sem("fb_sel_ready"), sem("fb_summed"), sem("fb_added"), sem("fb_gathered"))
        acc_final = sem("acc_final")
        newton, pair_rooted = sem("newton"), sem("pair_rooted")
        xn2_ready = sem("xn2_ready")
        staged, acc_tp, x1_ready = sem("staged"), sem("acc_tp"), sem("x1_ready")
        stat2_ready = sem("stat2_ready")
        xl_tp, xlt_ready, xl_ready = sem("xl_tp"), sem("xlt_ready"), sem("xl_ready")
        mean_ready, logits_ready, route, exp_done = sem("mean_ready"), sem("logits_ready"), sem("route"), sem("exp_done")
        idx_ready = sem("idx_ready")
        w1_in_sem = sem("w1_in")
        w2_got = [sem(f"w2_got{e}") for e in range(TOP_K)]
        b2_got = sem("b2_got")
        wts_ready, wcol_ps, wcol_ready, b2_ps, b2_ready = (
            sem("wts_ready"), sem("wcol_ps"), sem("wcol_ready"), sem("b2_ps"), sem("b2_ready"))
        b1_tp, b1t_ready, b1s_ready = sem("b1_tp"), sem("b1t_ready"), sem("b1s_ready")
        w1hi_ready, w1lo_ready, w2s_ready, w2hi_ready, w2lo_ready = (
            sem("w1hi_ready"), sem("w1lo_ready"), sem("w2s_ready"), sem("w2hi_ready"), sem("w2lo_ready"))
        xshi_ready, xslo_ready = sem("xshi_ready"), sem("xslo_ready")
        ffn1_done, gelu_done, ghi_ready, glo_ready = sem("ffn1_done"), sem("gelu_done"), sem("ghi_ready"), sem("glo_ready")
        ffn2_done, xlb_ready, z_ready, stat3_ready, mv3_ready = (
            sem("ffn2_done"), sem("xlb_ready"), sem("z_ready"), sem("stat3_ready"), sem("mv3_ready"))
        rstd3_ready, zn_ready, o_ready = sem("rstd3_ready"), sem("zn_ready"), sem("o_ready")
        fin_step, o_by_dve = sem("fin_step"), sem("o_by_dve")
        out_written = [sem("out_written0"), sem("out_written1")]

        HALVES = (slice(0, D_FF // 2), slice(D_FF // 2, D_FF))
        LAST_TWO = ((0, NT - 2), (1, NT - 1))

        block = ctx.enter_context(nc.Block())

        def nop_waits(engine):
            engine.nop(nofuse=True)

        def flat(a):
            return a.rearrange("(c e) -> c e", e=CHUNK)

        @block.sync
        def _(sp):
            sp.dma_start(x[:, 0:2, :], x_in[0:2 * P, :].rearrange("(t p) d -> p t d", p=P)).then_inc(x01_in, 16)
            for c in range(NCG):
                if c == NCG // 2:
                    sp.dma_start(x[:, 2:4, :], x_in[2 * P:4 * P, :].rearrange("(t p) d -> p t d", p=P)
                                 ).then_inc(x23_in, 16)
                for kh in range(KH):
                    sp.dma_start(w_raw[:, c, kh, :].rearrange("p (r o) -> p r o", r=2),
                                 w_in[2 * c:2 * c + 2, kh * P:(kh + 1) * P, :].rearrange("r p o -> p r o")
                                 ).then_inc(w_in_sem[c], 16)
            def store_table(t, b):
                sp.wait_ge(even_out, NCG // 2 * (t + 1) + 2)
                sp.wait_ge(odd_out, NCG // 2 * (t + 1) + 2)
                sp.dma_start(table_tiles[t], t_stage[:, b, :]).then_inc(t_written[b], 16)

            def store_table_in_parts(t, b):
                for n in range(NCG // 2):
                    sp.wait_ge(even_out, NCG // 2 * t + n + 3)
                    sp.wait_ge(odd_out, NCG // 2 * t + n + 3)
                    part = slice(n * 1024, (n + 1) * 1024)
                    sp.dma_start(table_tiles[t][:, part], t_stage[:, b, part]).then_inc(t_written[b], 16)

            sp.wait_ge(w_in_sem[NCG - 1], 16 * KH)
            sp.dma_start(x[:, 4:NT - 1, :],
                         x_in[4 * P:(NT - 1) * P, :].rearrange("(t p) d -> p t d", p=P)).then_inc(x_in_sem, 16)
            sp.wait_ge(x_zeroed, 1)
            full = LAST // 16 * 16
            sp.dma_start(x[0:full, NT - 1, :], x_in[(NT - 1) * P:(NT - 1) * P + full, :]).then_inc(x_in_sem, 16)
            sp.dma_start(x[full:LAST, NT - 1, :], x_in[(NT - 1) * P + full:N_NODES, :]).then_inc(x_in_sem, 16)
            store_table(0, 0)
            store_table(1, 1)
            sp.wait_ge(rows_filled, 4)
            for rows, src in ((src_rows, src_in), (rel_rows, rel_in), (dst_rows, dst_in),
                              (norm_rows, norm_in.rearrange("e one -> (e one)"))):
                lo, end = NCH // 32 * 32, NCH - 1
                sp.dma_start(rows[0:lo, :], flat(src[0:lo * CHUNK])).then_inc(edges_in, 16)
                sp.dma_start(rows[lo:end, :], flat(src[lo * CHUNK:end * CHUNK])).then_inc(edges_in, 16)
                sp.dma_start(rows[end:NCH, 0:TAIL], src[end * CHUNK:N_EDGES].unsqueeze(0)).then_inc(edges_in, 16)
            sp.dma_start(b1_rows[:], b1_in.rearrange("e (j p) -> (e j) p", p=P)).then_inc(consts_in, 16)
            sp.dma_start(wr[:], wr_in.rearrange("(h p) e -> p h e", p=P)).then_inc(consts_in, 16)
            sp.dma_start(br[:], br_in.unsqueeze(0)).then_inc(consts_in, 16)
            sp.dma_start(gamma[:], gamma_in.unsqueeze(0).to_broadcast([P, D])).then_inc(bc_in, 16)
            sp.dma_start(beta[:], beta_in.unsqueeze(0).to_broadcast([P, D])).then_inc(bc_in, 16)

            with sp.Fori(1, NT // 2) as i:
                for b in range(2):
                    store_table(2 * i + b, b)
            store_table_in_parts(NT - 1, 0)

            sp.wait_ge(chunk_summed, NCH // 2 + SLOTS)
            for e in range(N_EXPERTS):
                sp.dma_start(w1_all[:, e, :, :], w1_in[e].rearrange("(h p) f -> p h f", p=P)).then_inc(w1_in_sem, 16)

            sp.wait_ge(idx_ready, 1)
            for k in range(TOP_K):
                e = sp.value_load(top_i[0:1, k:k + 1], min_val=0, max_val=N_EXPERTS - 1)
                sp.dma_start(w2_raw[:, k * NF:(k + 1) * NF, :], w2_in.rearrange("e (j p) d -> e p j d", p=P)[e]
                             ).then_inc(w2_got[k], 16)
                sp.dma_start(b2_pair[0:1, k, :], b2_in[bass.ds(e, 1), :]).then_inc(b2_got, 16)

            def store_out(gi, b, full_group):
                if isinstance(gi, int) and gi == NG - 2:
                    sp.wait_ge(o_by_dve, 3)
                elif isinstance(gi, int) and gi == NG - 1:
                    sp.wait_ge(o_ready, NG - 1)
                else:
                    sp.wait_ge(o_ready, gi + 1)
                if full_group:
                    sp.dma_start(out[bass.ds(gi * TG, TG), :].rearrange("(s p) d -> p s d", p=P),
                                 o[:, b, :, :]).then_inc(out_written[b], 16)
                else:
                    sp.dma_start(out[gi * TG:gi * TG + full, :], o[0:full, b, 0, :]).then_inc(out_written[b], 16)
                    sp.dma_start(out[gi * TG + full:N_NODES, :], o[full:LAST, b, 0, :]).then_inc(out_written[b], 16)

            with sp.Fori(0, NG // 2 - 1) as i:
                for b in range(2):
                    store_out(2 * i + b, b, True)
            store_out(NG - 3, 0, True)
            store_out(NG - 2, 1, True)
            store_out(NG - 1, 0, False)
            sp.wait_ge(out_written[0], 16 * (NG // 2) + 32)
            sp.wait_ge(out_written[1], 16 * (NG // 2))

        @block.gpsimd
        def _(pool):
            steps = [0]

            def after(ins):
                steps[0] += 1
                ins.then_inc(pool_step, 1)
                pool.wait_ge(pool_step, steps[0])

            nc.gpsimd.memset(x[:, NT - 1, :], 0.0).then_inc(x_zeroed, 1)
            pool.wait_ge(x_zeroed, 1)
            lo = NCH // 32 * 32
            nc.gpsimd.memset(src_rows[lo:NCH, :], 0).then_inc(rows_filled, 1)
            nc.gpsimd.memset(rel_rows[lo:NCH, :], 0).then_inc(rows_filled, 1)
            nc.gpsimd.memset(norm_rows[lo:NCH, :], 0.0).then_inc(rows_filled, 1)
            nc.gpsimd.memset(dst_rows[lo:NCH, :], NO_NODE).then_inc(rows_filled, 1)
            pool.wait_ge(rows_filled, 4)
            after(nc.gpsimd.memset(ident[:], 0.0))
            nc.gpsimd.affine_select(out=ident[:], in_=ident[:], compare_op=ALU.not_equal, fill=1.0, base=0,
                                    pattern=[[-1, P]], channel_multiplier=1).then_inc(ident_ready, 1)
            after(nc.gpsimd.memset(minus_half[:], -0.5))
            after(nc.gpsimd.memset(eps[:], LN_EPS))

            def rstd_pool(var, out_ap, n, half, ready, step_at, count=1):
                nc.gpsimd.tensor_tensor(var_eps[:, 0:n], var, eps[:, 0:n], ALU.add).then_inc(pool_step, 1)
                pool.wait_ge(pool_step, step_at)
                nc.gpsimd.tensor_tensor(out_ap, var_eps[:, 0:n], half, ALU.pow).then_inc(ready, count)

            pool.wait_ge(mv_ready, 2)
            steps[0] += 1
            rstd_pool(mv1[:, :, 1], rstd1[:, 0:2], 2, minus_half[:, 0:2], rstd_ready, steps[0], 2)
            for c in range(1, NCG, 2):
                pool.wait_ge(w_in_sem[c], 16 * KH)
                pool.wait_ge(whi_ready, c + 1)
                nc.gpsimd.tensor_tensor(w_lo[:, c, :, :], w_raw[:, c, :, :], w_hi[:, c, :, :].bitcast(F32),
                                        ALU.subtract).then_inc(wlo_odd, 1)
            nc.gpsimd.memset(ones[:], 1.0)
            nc.gpsimd.iota(thr_i[:, 0:1], [[0, 1]], base=0, channel_multiplier=1)
            nc.gpsimd.iota(iota_i[:], [[1, WIN]], base=0, channel_multiplier=0).then_inc(consts_ready, 1)
            pool.wait_ge(consts_ready, 1)
            nc.gpsimd.tensor_copy(iota[:], iota_i[:]).then_inc(consts_ready, 1)
            base_steps = steps[0]

            def rstd_tile(t, b):
                pool.wait_ge(mv_ready, t + 1)
                pool.wait_ge(rstd_ready, t)
                rstd_pool(mv1[:, b, 1:2], rstd1[:, bass.ds(t, 1)], 1, minus_half[:, 0:1], rstd_ready,
                          t + (base_steps - 1))

            with pool.Fori(0, (NT - 3) // 4) as i:
                rstd_tile(2 * i + 2, 0)
                rstd_tile(2 * i + 3, 1)
            steps[0] = base_steps + (NT - 3) // 4 * 2
            pool.wait_ge(edges_in, 4 * 3 * 16)
            nc.gpsimd.tensor_copy(srcf_rows[:], src_rows[:])
            nc.gpsimd.tensor_copy(relf_rows[:], rel_rows[:])
            after(nc.gpsimd.tensor_copy(dstf_rows[:], dst_rows[:]))
            after(nc.gpsimd.tensor_scalar(idxf_rows[:], srcf_rows[:], float(N_RELS), 0.0, ALU.mult, ALU.add))
            nc.gpsimd.tensor_tensor(idxf_rows[:], idxf_rows[:], relf_rows[:], ALU.add).then_inc(edge_math, 1)
            base_steps += 2
            with pool.Fori((NT - 3) // 4, (NT - 3) // 2) as i:
                rstd_tile(2 * i + 2, 0)
                rstd_tile(2 * i + 3, 1)
            rstd_tile(NT - 1, 0)
            nc.gpsimd.memset(acc[:], 0.0).then_inc(acc_zeroed, 1)
            steps[0] = base_steps + (NT - 2)

            pool.wait_ge(t_written[0], 16 * (NT // 2 + NCG // 2))
            pool.wait_ge(t_written[1], 16 * (NT // 2))
            pool.wait_ge(meta_tp, 4)

            def gather(slot, signal):
                nop_waits(pool)
                for j in range(CT):
                    nc.gpsimd.indirect_dma_start(
                        out=gath[:, slot, j, :], out_offset=None, in_=table,
                        in_offset=bass.IndirectOffsetOnAxis(ap=idx_now[:, slot, j:j + 1], axis=0)
                    ).then_inc(signal, 16)

            with pool.Fori(0, NCH // SLOTS) as i:
                for k in range(SLOTS):
                    pool.wait_ge(idx_now_ready, i * SLOTS + k + 1)
                    pool.wait_ge(chunk_summed, i * SLOTS + k + 1)
                    gather(k, gathered[k])

            pool.wait_ge(meta_copied, 5)
            for k in range(SLOTS):
                pool.wait_ge(gathered[k], 64 * (NCH // SLOTS))
            pool.wait_ge(chunk_summed, NCH + SLOTS)
            missed = pool.value_load(w0_row[0:1, NCH:NCH + 1], min_val=0, max_val=1)
            with pool.If(missed):
                with pool.Fori(0, NCH) as c:
                    pool.wait_ge(fb_summed, c * NFB + 1)
                    nc.gpsimd.tensor_copy(idx_now[:, 0, :], idx_col[:, bass.ds(c, 1), :].rearrange("p a b -> p (a b)")
                                          ).then_inc(fb_step, 1)
                    pool.wait_ge(fb_step, c + 1)
                    gather(0, fb_gathered)
                    pool.wait_ge(fb_gathered, c * 64 + 64)
            with pool.Else():
                pool.wait_ge(stat2_ready, NT * 2)
                nc.gpsimd.tensor_tensor(pair_root[:, 0, :], mv3[:, 0, :, 1], eps[:], ALU.add).then_inc(pair_rooted, 1)
                pool.wait_ge(pair_rooted, 1)
                nc.gpsimd.tensor_tensor(pair_root[:, 1, :], pair_root[:, 0, :], minus_half[:], ALU.pow
                                        ).then_inc(pair_rooted, 1)

            def add_b2(gi, n):
                cols = xl[:, bass.ds(gi * 2, n), :]
                nc.gpsimd.tensor_tensor(cols, cols, b2c[:].unsqueeze(1).to_broadcast([P, n, D]), ALU.add
                                        ).then_inc(xlb_ready, 1)

            def rstd_out(gi, b, n, step_at):
                pool.wait_ge(mv3_ready, gi + 1)
                rstd_pool(mv3[:, b, 0:n, 1], rstd3[:, bass.ds(gi * 2, n)], n, minus_half[:, 0:n],
                          rstd3_ready, step_at)

            def finish(gi, b, n):
                pool.wait_ge(zn_ready, gi + 1)
                if not isinstance(gi, int) or gi >= 2:
                    pool.wait_ge(out_written[b], gi * 8 - (8 * b))
                zb, ob = z[:, b, 0:n, :], o[:, b, 0:n, :]
                bc = lambda a: a[:].unsqueeze(1).to_broadcast([P, n, D])
                done = 2 * (NG - 2) if isinstance(gi, int) and gi == NG - 1 else gi * 2
                nc.gpsimd.tensor_tensor(ob, zb, bc(gamma), ALU.mult).then_inc(fin_step, 1)
                pool.wait_ge(fin_step, done + 1)
                nc.gpsimd.tensor_tensor(ob, ob, bc(beta), ALU.add).then_inc(fin_step, 1)
                pool.wait_ge(fin_step, done + 2)
                nc.gpsimd.tensor_tensor(ob, ob, x[:, bass.ds(gi * 2, n), :], ALU.add).then_inc(o_ready, 1)

            pool.wait_ge(xlt_ready, KH * NT + KH)
            nc.gpsimd.tensor_copy(xs_hi[:, 0, :, :], acc[:, :, 0:TG]).then_inc(xshi_ready, 1)
            nc.gpsimd.tensor_copy(xs_hi[:, 1, :, :], acc[:, :, TG:2 * TG]).then_inc(xshi_ready, 1)
            for k in range(TOP_K):
                pool.wait_ge(w2hi_ready, k + 1)
                half = slice(k * NF, k * NF + NF)
                nc.gpsimd.tensor_tensor(w2_lo[:, half, :], w2_raw[:, half, :], w2_hi[:, half, :].bitcast(F32),
                                        ALU.subtract).then_inc(w2lo_ready, 1)
            pool.wait_ge(b2_ready, 1)
            pool.wait_ge(bc_in, 32)
            pool.wait_ge(xl_ready, NT + 1)
            add_b2(0, 2)
            base_steps = steps[0]

            def step(gi, b, first=False):
                if not isinstance(gi, int) or gi + 2 < NG:
                    pool.wait_ge(ffn1_done, gi * NU + NU)
                    nc.gpsimd.tensor_copy(xs_hi[:, b, :, :], acc[:, :, bass.ds(gi * TG + 2 * TG, TG)]
                                          ).then_inc(xshi_ready, 1)
                if not isinstance(gi, int) or gi + 1 < NG:
                    add_b2(gi + 1, 1 if isinstance(gi, int) and gi + 1 == NG - 1 else 2)
                if not first:
                    finish(gi - 1, 1 - b, 2)
                rstd_out(gi, b, 1 if isinstance(gi, int) and gi == NG - 1 else 2, gi + (base_steps + 1))

            step(0, 0, first=True)
            step(1, 1)
            step(2, 0)
            with pool.Fori(1, 5) as i:
                step(2 * i + 1, 1)
                step(2 * i + 2, 0)
            step(11, 1)
            rstd_out(NG - 1, 0, 1, base_steps + NG)
            finish(NG - 1, 0, 1)

        @block.scalar
        def _(act):
            act.sem_inc(even_out, 2)
            act.sem_inc(gelu_done, NU)
            act.sem_inc(xlt_ready, KH)
            act.sem_inc(xl_ready, 1)
            def hi_part(t, b):
                act.wait_ge(tp_ready, t + 1)
                nc.scalar.activation(ht_hi[:, b, :], bank[4][:, 0:D], ACT.Copy).then_inc(hthi_ready, 1)

            def evacuate(t, b, c):
                act.wait_ge(mm_done, t * NCG + (c + 1))
                nc.scalar.activation(t_stage[:, b, c * 512:(c + 1) * 512], bank[c % 4][:], ACT.Copy
                                     ).then_inc(even_out, 1)

            act.wait_ge(w_in_sem[0], 16 * KH)
            nc.scalar.activation(w_hi[:, 0, :, :], w_raw[:, 0, :, :], ACT.Copy).then_inc(whi_ready, 1)
            hi_part(0, 0)
            for c in range(1, NCG):
                act.wait_ge(w_in_sem[c], 16 * KH)
                nc.scalar.activation(w_hi[:, c, :, :], w_raw[:, c, :, :], ACT.Copy).then_inc(whi_ready, 1)
                if c in (3, 5, 7):
                    evacuate(0, 0, c - 3)
            hi_part(1, 1)
            evacuate(0, 0, 6)

            def tile_a(t, b, last=False):
                if not isinstance(t, int) or t > b:
                    act.wait_ge(t_written[b], t * 8 - 8 * b)
                evacuate(t, b, 0)
                evacuate(t, b, 2)
                if not last:
                    hi_part(t + 1, 1 - b)
                evacuate(t, b, 4)
                evacuate(t, b, 6)

            tile_a(1, 1)
            tile_a(2, 0)
            with act.Fori(1, (NT - 3) // 2) as i:
                tile_a(2 * i + 1, 1)
                tile_a(2 * i + 2, 0)
            tile_a(NT - 2, 1)
            tile_a(NT - 1, 0, last=True)

            def tile_cols(b):
                return bank[b][:, 0:CT * NCH].rearrange("p (j c) -> p c j", j=CT)

            act.wait_ge(meta_tp, 1)
            nc.scalar.activation(idx_col[:], tile_cols(5), ACT.Copy).then_inc(idx_copied, 1)
            act.wait_ge(meta_tp, 2)
            nc.scalar.activation(norm_col[:], tile_cols(7), ACT.Copy).then_inc(meta_copied, 1)

            act.wait_ge(idx_copied, 1)

            def place_indices(i, ks=range(SLOTS)):
                for k in ks:
                    if not isinstance(i, int) or i > 0:
                        act.wait_ge(gathered[k], i * 64)
                    nc.scalar.activation(idx_now[:, k, :], idx_col[:, bass.ds(i * SLOTS + k, 1), :].rearrange(
                        "p a b -> p (a b)"), ACT.Copy).then_inc(idx_now_ready, 1)

            def stage(t):
                act.wait_ge(acc_tp, t + 1)
                nc.scalar.activation(acc_stage[:].rearrange("p (h n) -> p h n", h=KH),
                                     acc[:, :, bass.ds(t * P, P)], ACT.Copy).then_inc(staged, 1)

            def keep(t):
                act.wait_ge(xn2_ready, t + 1)
                nc.scalar.activation(xl[:, bass.ds(t, 1), :].rearrange("p a d -> p (a d)"), xn[:], ACT.Copy
                                     ).then_inc(xl_ready, 1)
                act.wait_ge(xl_tp, t + 2)
                for h in range(KH):
                    nc.scalar.activation(acc[:, h, bass.ds(t * P, P)], bank[3][:, h * P:(h + 1) * P], ACT.Copy,
                                         accum_out=mean_sum[:, h, bass.ds(t, 1)]).then_inc(xlt_ready, 1)

            act.wait_ge(meta_copied, 5)
            nc.scalar.activation(warm[:, 0:1], ident[0:1, 0:1], ACT.Exp)
            general = act.value_load(w0_row[0:1, NCH:NCH + 1], min_val=0, max_val=1)
            with act.If(general):
                place_indices(0)
                with act.Fori(1, NIT) as i:
                    place_indices(i)
                act.wait_ge(acc_final, 1)
                with act.Fori(0, NT) as t:
                    stage(t)
                    keep(t)
            with act.Else():
                place_indices(0)
                with act.Fori(1, LAG) as i:
                    place_indices(i)
                place_indices(LAG, (0, 1))
                with act.Fori(0, NIT - LAG - 1) as t:
                    place_indices(t + LAG, (2, 3))
                    act.wait_ge(acc_added, t * SLOTS + (LAG * SLOTS + 2))
                    stage(t)
                    place_indices(t + (LAG + 1), (0, 1))
                    keep(t)
                place_indices(NIT - 1, (2, 3))
                act.wait_ge(acc_added, (NIT - 1) * SLOTS + 2)
                stage(NIT - LAG - 1)
                keep(NIT - LAG - 1)
                act.wait_ge(acc_added, NCH + 2)
                for s, t in LAST_TWO:
                    nc.scalar.activation(pair_stage[:, s, :].rearrange("p (h n) -> p h n", h=KH),
                                         acc[:, :, t * P:(t + 1) * P], ACT.Copy).then_inc(staged, 1)
                for s, t in LAST_TWO:
                    act.wait_ge(xn2_ready, t + 1)
                    nc.scalar.activation(xl[:, t, :], pair_xn[:, s, :], ACT.Copy).then_inc(xl_ready, 1)
                for s, t in LAST_TWO:
                    act.wait_ge(xl_tp, t + 2)
                    for h in range(KH):
                        nc.scalar.activation(acc[:, h, t * P:(t + 1) * P], bank[3 + 4 * s][:, h * P:(h + 1) * P],
                                             ACT.Copy, accum_out=mean_sum[:, h, t:t + 1]).then_inc(xlt_ready, 1)
            act.wait_ge(b1_tp, 1)
            nc.scalar.activation(b1t[:], bank[4][:, 0:N_EXPERTS * NF], ACT.Copy).then_inc(b1t_ready, 1)

            act.wait_ge(route, 2)
            nc.scalar.activation(rt[:, 2, :], rt[:, 0, :], ACT.Exp, bias=rt[:, 1, 0:1], accum_out=rt[:, 3, 0:1]
                                 ).then_inc(exp_done, 1)
            act.wait_ge(route, 5)
            nc.scalar.activation(rt[:, 8, :], rt[:, 6, :], ACT.Exp, bias=rt[:, 7, 0:1], accum_out=rt[:, 9, 0:1]
                                 ).then_inc(exp_done, 1)
            act.wait_ge(route, 9)
            nc.scalar.activation(rt[:, 13, 0:TOP_K], rt[:, 11, 0:TOP_K], ACT.Exp, bias=rt[:, 12, 0:1],
                                 accum_out=rt[:, 14, 0:1]).then_inc(exp_done, 1)
            act.wait_ge(idx_ready, 1)
            act.wait_ge(w1_in_sem, 16 * N_EXPERTS)
            chosen = []
            for k in range(TOP_K):
                e = act.value_load(top_i[0:1, k:k + 1], min_val=0, max_val=N_EXPERTS - 1)
                for cols in HALVES:
                    nc.scalar.activation(w1_hi[:, k, :, cols], w1_all[:, bass.ds(e, 1), :, cols].rearrange(
                        "p e h f -> p (e h) f"), ACT.Copy).then_inc(w1hi_ready, 1)
                chosen.append(e)
            for k, e in enumerate(chosen):
                nc.scalar.activation(b1s[:, k * NF:(k + 1) * NF], b1t[:, bass.ds(e * NF, NF)], ACT.Copy
                                     ).then_inc(b1s_ready, 1)
            for k in range(TOP_K):
                act.wait_ge(w2s_ready, k + 1)
                half = slice(k * NF, k * NF + NF)
                nc.scalar.activation(w2_hi[:, half, :], w2_raw[:, half, :], ACT.Copy).then_inc(w2hi_ready, 1)
            nc.scalar.activation(warm[:, 1:2], rt[:, 11, 0:1], ACT.Gelu)
            act.wait_ge(b1s_ready, TOP_K)

            def gelu_group(gi, b):
                for u in range(NU):
                    act.wait_ge(ffn1_done, gi * NU + (u + 1))
                    act.wait_ge(glo_ready, gi * NU + (u + 1))
                    for v in range(2):
                        q = 2 * u + v
                        last = nc.scalar.activation(g[:, u % 2, v, :], bank[u][:, v * TG:(v + 1) * TG], ACT.Gelu,
                                                    bias=b1s[:, q:q + 1])
                    last.then_inc(gelu_done, 1)
                    act.wait_ge(gelu_done, gi * NU + (NU + u + 1))
                    if u == 0:
                        act.wait_ge(ffn2_done, gi * 2)
                    nc.scalar.activation(g_hi[:, b, 2 * u:2 * u + 2, :], g[:, u % 2, :, :], ACT.Copy
                                         ).then_inc(ghi_ready, 1)

            gelu_group(0, 0)
            gelu_group(1, 1)
            with act.Fori(0, 5) as i:
                gelu_group(2 * i + 2, 0)
                gelu_group(2 * i + 3, 1)
            gelu_group(12, 0)

        @block.vector
        def _(dve):
            dve.sem_inc(odd_out, 2)
            dve.sem_inc(acc_added, 2)
            dve.sem_inc(glo_ready, 2)
            dve.sem_inc(z_ready, 2)
            dve.sem_inc(x1_ready, 1)

            def stats(t, b):
                nc.vector.bn_stats(stat[:, b, :], x[:, bass.ds(t, 1), :].rearrange("p a d -> p (a d)")
                                   ).then_inc(stat_ready, 1)
                dve.wait_ge(stat_ready, t + 1)
                nop_waits(dve)
                nc.vector.bn_aggr(mv1[:, b, :], stat[:, b, :]).then_inc(mv_ready, 1)

            def norm(t, b):
                dve.wait_ge(rstd_ready, t + 1)
                dve.wait_ge(tp_ready, t)
                nc.vector.tensor_scalar(xn[:], x[:, bass.ds(t, 1), :].rearrange("p a d -> p (a d)"),
                                        mv1[:, b, 0:1], rstd1[:, bass.ds(t, 1)],
                                        ALU.subtract, ALU.mult).then_inc(xn_ready, 1)

            def lo_part(t, b):
                dve.wait_ge(hthi_ready, t + 1)
                nc.vector.tensor_tensor(ht_lo[:, b, :], bank[4][:, 0:D], ht_hi[:, b, :].bitcast(F32), ALU.subtract
                                        ).then_inc(htlo_ready, 1)

            def evacuate(t, b, c):
                dve.wait_ge(mm_done, t * NCG + (c + 1))
                nc.vector.tensor_copy(t_stage[:, b, c * 512:(c + 1) * 512], bank[c % 4][:]).then_inc(odd_out, 1)

            dve.wait_ge(x01_in, 16)
            stats(0, 0)
            stats(1, 1)
            norm(0, 0)

            def w_low(c):
                dve.wait_ge(w_in_sem[c], 16 * KH)
                dve.wait_ge(whi_ready, c + 1)
                nc.vector.tensor_tensor(w_lo[:, c, :, :], w_raw[:, c, :, :], w_hi[:, c, :, :].bitcast(F32),
                                        ALU.subtract).then_inc(wlo_even, 1)

            w_low(0)
            lo_part(0, 0)
            w_low(2)
            norm(1, 1)
            w_low(4)
            evacuate(0, 0, 1)
            w_low(6)
            evacuate(0, 0, 3)
            evacuate(0, 0, 5)
            lo_part(1, 1)
            evacuate(0, 0, 7)

            def tile_a(t, b, last=False, between=()):
                def aside(i):
                    if between:
                        between[i]()

                if not last:
                    stats(t + 1, 1 - b)
                if not isinstance(t, int) or t > b:
                    dve.wait_ge(t_written[b], t * 8 - 8 * b)
                evacuate(t, b, 1)
                if not last:
                    norm(t + 1, 1 - b)
                aside(0)
                evacuate(t, b, 3)
                aside(1)
                evacuate(t, b, 5)
                if not last:
                    lo_part(t + 1, 1 - b)
                aside(2)
                evacuate(t, b, 7)
                aside(3)

            dve.wait_ge(x23_in, 16)
            tile_a(1, 1)
            tile_a(2, 0)
            dve.wait_ge(x_in_sem, 48)
            with dve.Fori(1, (NT - 3) // 2) as i:
                tile_a(2 * i + 1, 1)
                tile_a(2 * i + 2, 0)
            meta = [0]

            def after(ins):
                meta[0] += 1
                ins.then_inc(dve_meta, 1)
                dve.wait_ge(dve_meta, meta[0])

            def first_nodes():
                dve.wait_ge(edge_math, 1)
                after(nc.vector.tensor_reduce(w0_rows[:, 0:1], dstf_rows[:], AX.X, ALU.min))

            def places():
                after(nc.vector.tensor_scalar(pos_rows[:], dstf_rows[:], w0_rows[:, 0:1], None, ALU.subtract))
                after(nc.vector.tensor_scalar(srcf_rows[:], dstf_rows[:], float(NO_NODE // 2), None, ALU.is_lt))

            def misses():
                after(nc.vector.scalar_tensor_tensor(out=miss_rows[:], in0=pos_rows[:], scalar=float(WIN),
                                                     in1=srcf_rows[:], op0=ALU.is_ge, op1=ALU.mult))
                after(nc.vector.tensor_reduce(w0_rows[:, 1:2], miss_rows[:], AX.X, ALU.max))

            def order():
                dve.wait_ge(consts_ready, 1)
                after(nc.vector.tensor_scalar(thr_i[:, 1:2], thr_i[:, 0:1], SLOTS.bit_length() - 1, None,
                                              ALU.arith_shift_right))
                after(nc.vector.tensor_scalar(thr[:, 0:1], thr_i[:, 1:2], float(P), float(P * (1 - LAG)), ALU.mult,
                                              ALU.add))
                after(nc.vector.tensor_tensor(thr[:, 1:2], w0_rows[:, 0:1], thr[:, 0:1], ALU.is_lt))
                after(nc.vector.tensor_tensor(w0_rows[:, 1:2], w0_rows[:, 1:2], thr[:, 1:2], ALU.max))

            tile_a(NT - 2, 1, between=(first_nodes, places, misses, order))
            tile_a(NT - 1, 0, last=True)

            def tile_cols(b):
                return bank[b][:, 0:CT * NCH].rearrange("p (j c) -> p c j", j=CT)

            dve.wait_ge(meta_tp, 3)
            nc.vector.tensor_copy(rel_pos[:], tile_cols(6)).then_inc(meta_copied, 1)
            dve.wait_ge(meta_tp, 4)
            nc.vector.tensor_copy(dst_col[:], tile_cols(5)).then_inc(meta_copied, 1)
            dve.wait_ge(meta_tp, 5)
            nc.vector.tensor_copy(w0_row[:, 0:NCH], bank[4][0:1, 256:256 + NCH]).then_inc(meta_copied, 1)
            nc.vector.tensor_scalar(w0_row[:, NCH:NCH + 1], bank[4][0:1, 256 + NCH:257 + NCH], 0.5, None, ALU.is_gt
                                    ).then_inc(meta_copied, 1)

            dve.wait_ge(meta_copied, 5)
            dve.wait_ge(consts_ready, 2)
            dve.wait_ge(acc_zeroed, 1)

            def weigh(i, ks=range(SLOTS)):
                for k in ks:
                    c = bass.ds(i * SLOTS + k, 1)
                    for j in range(CT):
                        last = nc.vector.tensor_scalar(sel[:, k, j, :], iota[:], rel_pos[:, c, j], norm_col[:, c, j],
                                                       ALU.is_equal, ALU.mult)
                    last.then_inc(sel_ready, 1)

            def add_chunk(i, k):
                w0 = dve.value_load(w0_row[0:1, bass.ds(i * SLOTS + k, 1)], min_val=0, max_val=N_NODES - 1)
                dve.wait_ge(chunk_summed, i * SLOTS + (SLOTS + k + 1))
                dve.wait_ge(acc_added, i * SLOTS + (k + 2))
                window = acc[:, :, bass.ds(w0, WIN)]
                nc.vector.tensor_tensor(window, window, bank[6 + k % 2][:, 0:KH * WIN].rearrange(
                    "p (h w) -> p h w", h=KH), ALU.add).then_inc(acc_added, 1)

            def chunks(i):
                weigh(i)
                for k in range(SLOTS):
                    add_chunk(i, k)

            def reciprocal_root(t, var, ve, y, m):
                n = [0]

                def then(ins):
                    n[0] += 1
                    ins.then_inc(newton, 1)
                    dve.wait_ge(newton, t * NEWTON + n[0])

                then(nc.vector.tensor_scalar(ve, var, LN_EPS, None, ALU.add))
                then(nc.vector.tensor_scalar(y.bitcast(I32), ve.bitcast(I32), -0.5, 1597463007.0, ALU.mult, ALU.add))
                for _ in range(3):
                    then(nc.vector.tensor_tensor(m, y, y, ALU.mult))
                    then(nc.vector.scalar_tensor_tensor(out=m, in0=m, scalar=-0.5, in1=ve, op0=ALU.mult, op1=ALU.mult))
                    then(nc.vector.scalar_tensor_tensor(out=y, in0=m, scalar=1.5, in1=y, op0=ALU.add, op1=ALU.mult))
                assert n[0] == NEWTON

            def add_messages(t):
                dve.wait_ge(acc_tp, t + 2)
                tile = x[:, bass.ds(t, 1), :].rearrange("p a d -> p (a d)")
                nc.vector.tensor_tensor(tile, tile, bank[5][:, 0:D], ALU.add).then_inc(x1_ready, 1)
                dve.wait_ge(x1_ready, t + 2)
                nop_waits(dve)
                nc.vector.bn_stats(stat[:, 0, :], tile).then_inc(stat2_ready, 1)
                dve.wait_ge(stat2_ready, t * 2 + 1)
                nop_waits(dve)
                nc.vector.bn_aggr(mv2[:], stat[:, 0, :]).then_inc(stat2_ready, 1)

            def normalise(t):
                dve.wait_ge(stat2_ready, t * 2 + 2)
                y = root[:, 1:2]
                reciprocal_root(t, mv2[:, 1:2], root[:, 0:1], y, root[:, 2:3])
                dve.wait_ge(xl_tp, t + 1)
                dve.wait_ge(xl_ready, t + 1)
                nc.vector.tensor_scalar(xn[:], x[:, bass.ds(t, 1), :].rearrange("p a d -> p (a d)"),
                                        mv2[:, 0:1], y, ALU.subtract, ALU.mult).then_inc(xn2_ready, 1)

            general = dve.value_load(w0_row[0:1, NCH:NCH + 1], min_val=0, max_val=1)
            with dve.If(general):
                with dve.Fori(0, NIT) as i:
                    chunks(i)
                dve.wait_ge(acc_added, NCH + 2)
                dve.wait_ge(t_written[0], 16 * (NT // 2 + NCG // 2))
                dve.wait_ge(t_written[1], 16 * (NT // 2))
                line = fb_iota[:].rearrange("p a b -> p (a b)")
                nc.vector.tensor_copy(line[:, 0:WIN], iota[:]).then_inc(fb_added, 1)
                done, filled = 1, WIN
                dve.wait_ge(fb_added, done)
                while filled < NFB * FBW:
                    n = min(filled, NFB * FBW - filled)
                    nc.vector.tensor_scalar(line[:, filled:filled + n], line[:, 0:n], float(filled), None, ALU.add
                                            ).then_inc(fb_added, 1)
                    done += 1
                    dve.wait_ge(fb_added, done)
                    filled += n
                nc.vector.scalar_tensor_tensor(out=fb_norm[:], in0=rel_pos[:], scalar=float(WIN), in1=norm_col[:],
                                               op0=ALU.is_ge, op1=ALU.mult).then_inc(fb_added, 1)
                done += 1
                dve.wait_ge(fb_added, done)
                with dve.Fori(0, NCH) as c:
                    with dve.Fori(0, NFB) as w:
                        s = c * NFB + w
                        for j in range(CT):
                            last = nc.vector.tensor_scalar(
                                fb_sel[:, j, :], fb_iota[:, bass.ds(w, 1), :].rearrange("p a b -> p (a b)"),
                                dst_col[:, bass.ds(c, 1), j], fb_norm[:, bass.ds(c, 1), j], ALU.is_equal, ALU.mult)
                        last.then_inc(fb_sel_ready, 1)
                        dve.wait_ge(fb_summed, s + 2)
                        for h in range(KH):
                            cols = acc[:, h, bass.ds(w * FBW, FBW)]
                            nc.vector.tensor_tensor(cols, cols, bank[6 + h][:, 0:FBW], ALU.add
                                                    ).then_inc(fb_added, 1)
                        dve.wait_ge(fb_added, s * KH + (done + KH))
                dve.drain().then_inc(acc_final, 1)
                with dve.Fori(0, NT) as t:
                    add_messages(t)
                    normalise(t)
            with dve.Else():
                with dve.Fori(0, LAG) as i:
                    chunks(i)
                with dve.Fori(0, NIT - LAG) as t:
                    weigh(t + LAG, (0, 1))
                    add_messages(t)
                    weigh(t + LAG, (2,))
                    normalise(t)
                    add_chunk(t + LAG, 0)
                    weigh(t + LAG, (3,))
                    for k in range(1, SLOTS):
                        add_chunk(t + LAG, k)
                for s, t in LAST_TWO:
                    dve.wait_ge(acc_tp, t + 2)
                    nc.vector.tensor_tensor(x[:, t, :], x[:, t, :], bank[5 + s][:, 0:D], ALU.add).then_inc(x1_ready, 1)
                for s, t in LAST_TWO:
                    dve.wait_ge(x1_ready, t + 2)
                    nc.vector.bn_stats(stat[:, s, :], x[:, t, :]).then_inc(stat2_ready, 1)
                dve.wait_ge(stat2_ready, (NT - 2) * 2 + 2)
                for s, t in LAST_TWO:
                    nc.vector.bn_aggr(mv3[:, 0, s, :], stat[:, s, :]).then_inc(stat2_ready, 1)
                dve.wait_ge(pair_rooted, 2)
                for s, t in LAST_TWO:
                    nc.vector.tensor_scalar(pair_xn[:, s, :], x[:, t, :], mv3[:, 0, s, 0:1], pair_root[:, 1, s:s + 1],
                                            ALU.subtract, ALU.mult).then_inc(xn2_ready, 1)

            n_route = [0]

            def routed(ins):
                n_route[0] += 1
                ins.then_inc(route, 1)
                dve.wait_ge(route, n_route[0])

            V = nc.vector

            def token_lo(gi, b):
                dve.wait_ge(xshi_ready, gi + 1)
                V.tensor_tensor(xs_lo[:, b, :, :], acc[:, :, bass.ds(gi * TG, TG)], xs_hi[:, b, :, :].bitcast(F32),
                                ALU.subtract).then_inc(xslo_ready, 1)

            dve.wait_ge(xlt_ready, KH * NT + KH)
            V.tensor_reduce(mean[:], mean_sum[:], AX.X, ALU.add).then_inc(mean_ready, 1)
            dve.wait_ge(logits_ready, 1)
            dve.wait_ge(consts_in, 48)
            routed(V.scalar_tensor_tensor(out=rt[:, 0, :], in0=bank[5][0:1, 0:N_EXPERTS], scalar=1.0 / N_NODES,
                                          in1=br[:], op0=ALU.mult, op1=ALU.add))
            routed(V.tensor_reduce(rt[:, 1, 0:1], rt[:, 0, :], AX.X, ALU.max, negate=True))
            dve.wait_ge(exp_done, 1)
            routed(V.reciprocal(rt[:, 3, 1:2], rt[:, 3, 0:1]))
            routed(V.tensor_scalar(rt[:, 6, :], rt[:, 2, :], rt[:, 3, 1:2], CAPACITY / N_NODES, ALU.mult, ALU.min))
            routed(V.tensor_reduce(rt[:, 7, 0:1], rt[:, 6, :], AX.X, ALU.max, negate=True))
            token_lo(0, 0)
            dve.wait_ge(exp_done, 2)
            routed(V.reciprocal(rt[:, 9, 1:2], rt[:, 9, 0:1]))
            routed(V.tensor_scalar(rt[:, 10, :], rt[:, 8, :], rt[:, 9, 1:2], None, ALU.mult))
            routed(V.max(rt[:, 11, :], rt[:, 10, :]))
            V.max_index(top_i[:], rt[:, 11, :], rt[:, 10, :]).then_inc(idx_ready, 1)
            routed(V.tensor_scalar(rt[:, 12, 0:1], rt[:, 11, 0:1], -1.0, None, ALU.mult))
            token_lo(1, 1)
            dve.wait_ge(exp_done, 3)
            routed(V.reciprocal(rt[:, 14, 1:2], rt[:, 14, 0:1]))
            dve.wait_ge(consts_ready, 1)
            for k in range(TOP_K):
                routed(V.tensor_scalar(rt[:, 15, k:k + 1], rt[:, 13, k:k + 1], rt[:, 14, 1:2], None, ALU.mult))
            for k in range(TOP_K):
                V.tensor_scalar(w_rows[:, k, :], ones[0:1, :], rt[:, 15, k:k + 1], None, ALU.mult).then_inc(wts_ready, 1)

            def w1_lo_part(k):
                e = dve.value_load(top_i[0:1, k:k + 1], min_val=0, max_val=N_EXPERTS - 1)
                for i, cols in enumerate(HALVES):
                    dve.wait_ge(w1hi_ready, 2 * k + i + 1)
                    V.tensor_tensor(w1_lo[:, k, :, cols], w1_all[:, bass.ds(e, 1), :, cols].rearrange(
                        "p e h f -> p (e h) f"), w1_hi[:, k, :, cols].bitcast(F32), ALU.subtract
                                    ).then_inc(w1lo_ready, 1)

            dve.wait_ge(idx_ready, 1)
            w1_lo_part(0)
            dve.wait_ge(wcol_ps, 1)
            V.tensor_copy(w_cols[:], bank[5][:, 16:16 + TOP_K]).then_inc(wcol_ready, 1)
            dve.wait_ge(wcol_ready, 1)
            for k in range(TOP_K):
                dve.wait_ge(w2_got[k], 16)
                half = w2_raw[:, k * NF:(k + 1) * NF, :]
                V.tensor_scalar(half, half, w_cols[:, k:k + 1], None, ALU.mult).then_inc(w2s_ready, 1)
                if k == 0:
                    w1_lo_part(1)

            def gelu_lo(gi, b, u):
                dve.wait_ge(ghi_ready, gi * NU + (u + 1))
                V.tensor_tensor(g_lo[:, b, 2 * u:2 * u + 2, :], g[:, u % 2, :, :],
                                g_hi[:, b, 2 * u:2 * u + 2, :].bitcast(F32), ALU.subtract).then_inc(glo_ready, 1)

            def residual(gi, b, n):
                if not isinstance(gi, int) or gi >= 2:
                    dve.wait_ge(o_ready, gi - 1)
                dve.wait_ge(xlb_ready, gi + 1)
                for s in range(n):
                    dve.wait_ge(ffn2_done, gi * 2 + (s + 1 + 2))
                    V.tensor_tensor(z[:, b, s, :], bank[4 + s][:, 0:D],
                                    xl[:, bass.ds(gi * 2 + s, 1), :].rearrange("p a d -> p (a d)"), ALU.add
                                    ).then_inc(z_ready, 1)
                for s in range(n):
                    dve.wait_ge(z_ready, gi * 2 + (s + 1 + 2))
                    V.bn_stats(stat[:, s, :], z[:, b, s, :]).then_inc(stat3_ready, 1)
                dve.wait_ge(stat3_ready, gi * 2 + n)
                nop_waits(dve)
                for s in range(n):
                    last = V.bn_aggr(mv3[:, b, s, :], stat[:, s, :])
                last.then_inc(mv3_ready, 1)

            def norm_out(gi, b, n):
                dve.wait_ge(rstd3_ready, gi + 1)
                for s in range(n):
                    last = V.tensor_scalar(z[:, b, s, :], z[:, b, s, :], mv3[:, b, s, 0:1],
                                           rstd3[:, bass.ds(gi * 2 + s, 1)], ALU.subtract, ALU.mult)
                last.then_inc(zn_ready, 1)

            for u in range(NU):
                gelu_lo(0, 0, u)
            dve.wait_ge(b2_ps, 1)
            V.tensor_copy(b2c[:], bank[6][:, 0:D]).then_inc(b2_ready, 1)

            def step(gi, b, first=False):
                if not isinstance(gi, int) or gi + 1 < NG:
                    gelu_lo(gi + 1, 1 - b, 0)
                    gelu_lo(gi + 1, 1 - b, 1)
                if not first:
                    norm_out(gi - 1, 1 - b, 2)
                if not isinstance(gi, int) or gi + 1 < NG:
                    gelu_lo(gi + 1, 1 - b, 2)
                    gelu_lo(gi + 1, 1 - b, 3)
                if not isinstance(gi, int) or gi + 2 < NG:
                    token_lo(gi + 2, b)
                residual(gi, b, 1 if isinstance(gi, int) and gi == NG - 1 else 2)

            step(0, 0, first=True)
            step(1, 1)
            step(2, 0)
            with dve.Fori(1, 5) as i:
                step(2 * i + 1, 1)
                step(2 * i + 2, 0)
            step(11, 1)
            step(12, 0)
            dve.wait_ge(bc_in, 32)
            dve.wait_ge(zn_ready, NG - 1)
            dve.wait_ge(out_written[1], 16 * (NG // 2 - 1))
            both = lambda a: a[:].unsqueeze(1).to_broadcast([P, 2, D])
            V.tensor_tensor(o[:, 1, :, :], z[:, 1, :, :], both(gamma), ALU.mult).then_inc(o_by_dve, 1)
            norm_out(12, 0, 1)
            dve.wait_ge(o_by_dve, 1)
            V.tensor_tensor(o[:, 1, :, :], o[:, 1, :, :], both(beta), ALU.add).then_inc(o_by_dve, 1)
            dve.wait_ge(o_by_dve, 2)
            V.tensor_tensor(o[:, 1, :, :], o[:, 1, :, :], x[:, NT - 3:NT - 1, :], ALU.add).then_inc(o_by_dve, 1)

        @block.tensor
        def _(pe):
            pe.sem_inc(chunk_summed, SLOTS)
            pe.sem_inc(ffn2_done, 2)
            pe.sem_inc(acc_tp, 1)
            pe.sem_inc(xl_tp, 1)
            pe.sem_inc(fb_summed, 1)
            mm = nc.tensor.matmul

            def split_product(out_ap, a_hi, a_lo, b_hi, b_lo, first, last):
                mm(out_ap, a_lo, b_hi, start=first, stop=False)
                mm(out_ap, a_hi, b_lo, start=False, stop=False)
                return mm(out_ap, a_hi, b_hi, start=False, stop=last)

            def transposes(t, ready, src, bank_ap, done):
                pe.wait_ge(ready, t + 1)
                for h in range(KH):
                    last = nc.tensor.transpose(bank_ap[:, h * P:(h + 1) * P], src[:, h * P:(h + 1) * P], ident[:])
                last.then_inc(done, 1)

            def tile_a(t, b, last=False):
                pe.wait_ge(htlo_ready, t + 1)
                for c in range(NCG):
                    if c == NCG // 2 and not last:
                        transposes(t + 1, xn_ready, xn, bank[4], tp_ready)
                    pe.wait_ge(wlo_even if c % 2 == 0 else wlo_odd, c // 2 + 1)
                    pe.wait_ge(even_out if c % 2 == 0 else odd_out, t * (NCG // 2) + (c // 2 + 1))
                    for kh in range(KH):
                        rows = slice(kh * P, (kh + 1) * P)
                        done = split_product(bank[c % 4][:], ht_hi[:, b, rows], ht_lo[:, b, rows],
                                             w_hi[:, c, kh, :], w_lo[:, c, kh, :], kh == 0, kh == KH - 1)
                    done.then_inc(mm_done, 1)

            pe.wait_ge(ident_ready, 1)
            transposes(0, xn_ready, xn, bank[4], tp_ready)
            with pe.Fori(0, NT // 2) as i:
                for b in range(2):
                    tile_a(2 * i + b, b)
            tile_a(NT - 1, 0, last=True)

            def to_columns(rows, b, done):
                for j in range(CT):
                    last = nc.tensor.transpose(bank[b][:, j * NCH:(j + 1) * NCH], rows[:, j * P:(j + 1) * P],
                                               ident[0:NCH, 0:NCH])
                last.then_inc(done, 1)

            pe.wait_ge(edge_math, 1)
            to_columns(idxf_rows, 5, meta_tp)
            to_columns(norm_rows, 7, meta_tp)
            pe.wait_ge(dve_meta, 9)
            to_columns(pos_rows, 6, meta_tp)
            pe.wait_ge(idx_copied, 1)
            to_columns(dstf_rows, 5, meta_tp)
            pe.wait_ge(consts_ready, 1)
            mm(bank[4][0:1, 256:256 + NCH], w0_rows[:, 0:1], ident[0:NCH, 0:NCH], start=True, stop=True)
            mm(bank[4][0:1, 256 + NCH:257 + NCH], w0_rows[:, 1:2], ones[0:NCH, 0:1], start=True, stop=True
               ).then_inc(meta_tp, 1)

            pe.wait_ge(meta_copied, 5)
            pe.wait_ge(consts_in, 48)
            nc.tensor.transpose(bank[4][:, 0:N_EXPERTS * NF], b1_rows[:],
                                ident[0:N_EXPERTS * NF, 0:N_EXPERTS * NF]).then_inc(b1_tp, 1)

            def sum_chunks(i, ks):
                for k in ks:
                    pe.wait_ge(sel_ready, i * SLOTS + (k + 1))
                    pe.wait_ge(acc_added, i * SLOTS + (k + 1))
                    pe.wait_ge(gathered[k], i * 64 + 64)
                    for h in range(KH):
                        for j in range(CT):
                            last = mm(bank[6 + k % 2][:, h * WIN:(h + 1) * WIN], gath[:, k, j, h * P:(h + 1) * P],
                                      sel[:, k, j, :], start=j == 0, stop=j == CT - 1)
                    last.then_inc(chunk_summed, 1)

            def acc_tile(t):
                pe.wait_ge(x1_ready, t + 1)
                transposes(t, staged, acc_stage, bank[5], acc_tp)

            def xl_tile(t):
                pe.wait_ge(xlt_ready, t * KH + KH)
                transposes(t, xn2_ready, xn, bank[3], xl_tp)

            general = pe.value_load(w0_row[0:1, NCH:NCH + 1], min_val=0, max_val=1)
            with pe.If(general):
                with pe.Fori(0, NIT) as i:
                    sum_chunks(i, range(SLOTS))
                pe.wait_ge(acc_added, NCH + 2)
                with pe.Fori(0, NCH) as c:
                    with pe.Fori(0, NFB) as w:
                        pe.wait_ge(fb_gathered, c * 64 + 64)
                        pe.wait_ge(fb_sel_ready, c * NFB + w + 1)
                        for h in range(KH):
                            for j in range(CT):
                                last = mm(bank[6 + h][:, 0:FBW], gath[:, 0, j, h * P:(h + 1) * P], fb_sel[:, j, :],
                                          start=j == 0, stop=j == CT - 1)
                        last.then_inc(fb_summed, 1)
                with pe.Fori(0, NT) as t:
                    acc_tile(t)
                    xl_tile(t)
            with pe.Else():
                with pe.Fori(0, LAG) as i:
                    sum_chunks(i, range(SLOTS))
                with pe.Fori(0, NIT - LAG) as t:
                    acc_tile(t)
                    sum_chunks(t + LAG, (0, 1))
                    xl_tile(t)
                    sum_chunks(t + LAG, (2, 3))
                for s, t in LAST_TWO:
                    pe.wait_ge(x1_ready, NT - 1)
                    transposes(t, staged, pair_stage[:, s, :], bank[5 + s], acc_tp)
                for s, t in LAST_TWO:
                    pe.wait_ge(xlt_ready, (NT - 1) * KH)
                    transposes(t, xn2_ready, pair_xn[:, s, :], bank[3 + 4 * s], xl_tp)

            pe.wait_ge(mean_ready, 1)
            pe.wait_ge(b1t_ready, 1)
            for h in range(KH):
                last = mm(bank[5][0:1, 0:N_EXPERTS], mean[:, h:h + 1], wr[:, h, :], start=h == 0, stop=h == KH - 1)
            last.then_inc(logits_ready, 1)
            pe.wait_ge(wts_ready, TOP_K)
            mm(bank[5][:, 16:16 + TOP_K], ones[0:1, :], rt[:, 15, 0:TOP_K], start=True, stop=True).then_inc(wcol_ps, 1)
            def ffn1(gi, b):
                pe.wait_ge(xslo_ready, gi + 1)
                for u in range(NU):
                    if isinstance(gi, int) and gi == 0:
                        pe.wait_ge(w1lo_ready, u + 1)
                    pe.wait_ge(gelu_done, gi * NU + (u + 1))
                    for v in range(2):
                        k, f = divmod(2 * u + v, NF)
                        for kh in range(KH):
                            cols = slice(f * P, (f + 1) * P)
                            last = split_product(bank[u][:, v * TG:(v + 1) * TG], w1_hi[:, k, kh, cols],
                                                 w1_lo[:, k, kh, cols], xs_hi[:, b, kh, :], xs_lo[:, b, kh, :],
                                                 kh == 0, kh == KH - 1)
                    last.then_inc(ffn1_done, 1)

            def ffn2(gi, b, n):
                pe.wait_ge(glo_ready, gi * NU + (NU + 2))
                for s in range(n):
                    pe.wait_ge(z_ready, gi * 2 + (s + 1))
                    for q in range(NQ):
                        rows = slice(s * P, (s + 1) * P)
                        last = split_product(bank[4 + s][:, 0:D], g_hi[:, b, q, rows], g_lo[:, b, q, rows],
                                             w2_hi[:, q, :], w2_lo[:, q, :], q == 0, q == NQ - 1)
                    last.then_inc(ffn2_done, 1)

            ffn1(0, 0)
            pe.wait_ge(b2_got, 16 * TOP_K)
            for k in range(TOP_K):
                last = mm(bank[6][:, 0:D], w_rows[:, k, :], b2_pair[:, k, :], start=k == 0, stop=k == TOP_K - 1)
            last.then_inc(b2_ps, 1)
            ffn1(1, 1)
            pe.wait_ge(w2lo_ready, TOP_K)
            pe.wait_ge(b2_ready, 1)
            ffn2(0, 0, 2)
            with pe.Fori(0, 5) as i:
                ffn1(2 * i + 2, 0)
                ffn2(2 * i + 1, 1, 2)
                ffn1(2 * i + 3, 1)
                ffn2(2 * i + 2, 0, 2)
            ffn1(12, 0)
            ffn2(11, 1, 2)
            ffn2(12, 0, 1)


_INS = ['x', 'src', 'dst', 'edge_type_16', 'edge_weight1', 'L0_gnn_weight', 'L0_ffn_Wr', 'L0_ffn_br', 'L0_ffn_W1',
        'L0_ffn_b1', 'L0_ffn_W2', 'L0_ffn_b2', 'L0_ffn_gamma', 'L0_ffn_beta']


def build(nc, shapes):
    args = [nc.dram_tensor(f"in_{n}_dram", s, d, kind="ExternalInput").ap() for n, (s, d) in shapes.items()]
    args.append(nc.dram_tensor("out_0_dram", (N_NODES, D), F32, kind="ExternalOutput").ap())
    gnn_ffn(nc, *args)


def kernel(**inputs):
    import concourse.bacc as _bacc
    from concourse.bass_utils import run_bass_kernel_spmd as _run

    nc = _bacc.Bacc("TRN2", target_bir_lowering=False, num_devices=1)
    arrays = {f"in_{n}_dram": np.ascontiguousarray(inputs[n]) for n in _INS}
    build(nc, {n: (arrays[f"in_{n}_dram"].shape, mybir.dt.from_np(arrays[f"in_{n}_dram"].dtype)) for n in _INS})
    r = _run(nc, [arrays], core_ids=[0])
    return r.results[0]["out_0_dram"]
```
